# Optimizing a Trainium2 kernel written in Bass

```python
import numpy as np
import jax
import jax.numpy as jnp

def _softmax(x, axis=-1):
    return jax.nn.softmax(x, axis=axis)

def _gelu(x):
    return jax.nn.gelu(x, approximate=True)

def _silu(x):
    return jax.nn.silu(x)

def _sigmoid(x):
    return jax.nn.sigmoid(x)

def _layernorm(x, axis=-1, eps=1e-05):
    m = jnp.mean(x, axis=axis, keepdims=True)
    v = jnp.var(x, axis=axis, keepdims=True)
    return (x - m) / jnp.sqrt(v + eps)

def _scatter_add(tgt, idx, src, axis=0):
    return tgt.at[idx].add(src)

def _segment_sum(src, seg, n):
    return jax.ops.segment_sum(src, seg, n)
kernel_name = 'mk_adj_preln_d4_adj_r2_ff78d9'

def setup_inputs(seed: int=0):
    np.random.seed(seed)
    _w = jnp.asarray

    def _rec_inputs():
        import jax
        import jax.numpy as jnp
        _gk = jax.random.key(seed)
        x = -0.0001117 + 0.9999 * jax.random.normal(jax.random.fold_in(_gk, 1), (128, 128, 256), jnp.float32)
        _a = jax.random.bernoulli(jax.random.fold_in(_gk, 2), 0.0625, (128, 128))
        _a = jnp.logical_or(_a, jnp.swapaxes(_a, -1, -2))
        _a = jnp.logical_or(_a, jnp.eye(128, dtype=bool))
        adj = _a.astype(jnp.int32)
        return (x, adj)
    x, adj = _rec_inputs()

    def _L0_gnn_setup():
        import jax, jax.numpy as jnp
        import numpy as np
        B, N, F, F1 = (512, 75, 256, 128)
        NEG = -1000000000.0
        ALPHA = 0.2
        key = jax.random.key(seed)
        k1, k2, k3, k4 = jax.random.split(key, 4)
        X = jax.random.normal(k1, (B, N, F), dtype=jnp.float32)
        A = jax.random.randint(k2, (N, N), 0, 2, dtype=jnp.int32)
        W = jax.random.normal(k3, (F, F1), dtype=jnp.float32) * (1.0 / np.sqrt(F))
        a = jax.random.normal(k4, (2, F1, 1), dtype=jnp.float32) * (1.0 / np.sqrt(F1))
        return {'X': X, 'A': A, 'W': W, 'a': a}
    _L0_gnn_all = _L0_gnn_setup()
    _L0_gnn_in = {k: v for k, v in _L0_gnn_all.items() if k in ('W', 'a')}
    del _L0_gnn_all

    def _L1_gnn_setup():
        import jax, jax.numpy as jnp
        import numpy as np
        B, K, DIN, DOUT = (32, 64, 256, 256)
        key = jax.random.key(seed)
        k1, k2, k3, k4 = jax.random.split(key, 4)
        x = jax.random.normal(k1, (B, K, DIN), dtype=jnp.float32)
        adj = jax.random.randint(k2, (K, K), 0, 2, dtype=jnp.int32)
        W = jax.random.normal(k3, (DOUT, 2 * DIN), dtype=jnp.float32) * 0.02
        b = jax.random.normal(k4, (DOUT,), dtype=jnp.float32) * 0.02
        return {'x': x, 'adj': adj, 'W': W, 'b': b}
    _L1_gnn_all = _L1_gnn_setup()
    _L1_gnn_in = {k: v for k, v in _L1_gnn_all.items() if k in ('W', 'b')}
    del _L1_gnn_all

    def _L2_gnn_setup():
        import jax, jax.numpy as jnp
        import numpy as np
        D_MODEL = 256
        NUM_HEADS = 8
        D_HEAD = D_MODEL // NUM_HEADS
        B, N = (4, 1024)
        key = jax.random.key(seed)
        ks = jax.random.split(key, 10)
        s = 1.0 / np.sqrt(D_MODEL)
        inp = {'h': jax.random.normal(ks[0], (B, N, D_MODEL), dtype=jnp.float32), 'adj': jax.random.randint(ks[1], (N, N), 0, 2, dtype=jnp.int32), 'Wq': jax.random.uniform(ks[2], (D_MODEL, D_MODEL), jnp.float32, -s, s), 'bq': jax.random.uniform(ks[3], (D_MODEL,), jnp.float32, -s, s), 'Wk': jax.random.uniform(ks[4], (D_MODEL, D_MODEL), jnp.float32, -s, s), 'bk': jax.random.uniform(ks[5], (D_MODEL,), jnp.float32, -s, s), 'Wv': jax.random.uniform(ks[6], (D_MODEL, D_MODEL), jnp.float32, -s, s), 'bv': jax.random.uniform(ks[7], (D_MODEL,), jnp.float32, -s, s), 'Wo': jax.random.uniform(ks[8], (D_MODEL, D_MODEL), jnp.float32, -s, s), 'bo': jax.random.uniform(ks[9], (D_MODEL,), jnp.float32, -s, s)}
        return inp
    _L2_gnn_all = _L2_gnn_setup()
    _L2_gnn_in = {k: v for k, v in _L2_gnn_all.items() if k in ('Wq', 'bq', 'Wk', 'bk', 'Wv', 'bv', 'Wo', 'bo')}
    del _L2_gnn_all

    def _L3_gnn_setup():
        import jax, jax.numpy as jnp
        import numpy as np
        B, N, D = (8, 1024, 256)
        NEG_SLOPE = 0.2
        key = jax.random.key(seed)
        k1, k2, k3, k4, k5 = jax.random.split(key, 5)
        x = jax.random.normal(k1, (B, N, D), dtype=jnp.float32)
        adj = jax.random.randint(k2, (N, N), 0, 2, dtype=jnp.int32)
        adj = jnp.maximum(adj, jnp.eye(N, dtype=jnp.int32))
        W = jax.random.normal(k3, (D, D), dtype=jnp.float32) * (1.0 / np.sqrt(D))
        a_src = jax.random.normal(k4, (D,), dtype=jnp.float32) * (1.0 / np.sqrt(D))
        a_dst = jax.random.normal(k5, (D,), dtype=jnp.float32) * (1.0 / np.sqrt(D))
        return {'x': x, 'adj': adj, 'W': W, 'a_src': a_src, 'a_dst': a_dst}
    _L3_gnn_all = _L3_gnn_setup()
    _L3_gnn_in = {k: v for k, v in _L3_gnn_all.items() if k in ('W', 'a_src', 'a_dst')}
    del _L3_gnn_all
    return {'x': x, 'adj': adj, 'L0_gnn_W': _L0_gnn_in['W'], 'L0_gnn_a': _L0_gnn_in['a'], 'L1_gnn_W': _L1_gnn_in['W'], 'L1_gnn_b': _L1_gnn_in['b'], 'L2_gnn_Wq': _L2_gnn_in['Wq'], 'L2_gnn_bq': _L2_gnn_in['bq'], 'L2_gnn_Wk': _L2_gnn_in['Wk'], 'L2_gnn_bk': _L2_gnn_in['bk'], 'L2_gnn_Wv': _L2_gnn_in['Wv'], 'L2_gnn_bv': _L2_gnn_in['bv'], 'L2_gnn_Wo': _L2_gnn_in['Wo'], 'L2_gnn_bo': _L2_gnn_in['bo'], 'L3_gnn_W': _L3_gnn_in['W'], 'L3_gnn_a_src': _L3_gnn_in['a_src'], 'L3_gnn_a_dst': _L3_gnn_in['a_dst']}

def reference(x, adj, L0_gnn_W, L0_gnn_a, L1_gnn_W, L1_gnn_b, L2_gnn_Wq, L2_gnn_bq, L2_gnn_Wk, L2_gnn_bk, L2_gnn_Wv, L2_gnn_bv, L2_gnn_Wo, L2_gnn_bo, L3_gnn_W, L3_gnn_a_src, L3_gnn_a_dst):
    import jax
    import jax.numpy as jnp

    def _L0_gnn_ref(X, A, W, a):
        import jax, jax.numpy as jnp
        import numpy as np
        B, N, F, F1 = (512, 75, 256, 128)
        NEG = -1000000000.0
        ALPHA = 0.2
        h = jnp.einsum('bnf,fo->bno', X, W)
        att_self = jnp.einsum('bno,od->bnd', h, a[0])
        att_neigh = jnp.einsum('bno,od->bnd', h, a[1])
        e = att_self + jnp.swapaxes(att_neigh, 1, 2)
        e = jax.nn.leaky_relu(e, ALPHA)
        adj = A.astype(h.dtype)
        e = e + NEG * (1.0 - adj)[None, :, :]
        alpha = jax.nn.softmax(e, axis=-1)
        out = jnp.einsum('bij,bjo->bio', alpha, h)
        return jnp.concatenate([out, h], axis=-1)

    def _L1_gnn_ref(x, adj, W, b):
        import jax, jax.numpy as jnp
        import numpy as np
        B, K, DIN, DOUT = (32, 64, 256, 256)
        Din = x.shape[-1]
        Wi, Wj = (W[:, :Din], W[:, Din:])
        mi = jnp.einsum('bkd,od->bko', x, Wi)
        mj = jnp.einsum('bkd,od->bko', x, Wj)
        a = adj.astype(x.dtype)
        deg = a.sum(axis=1)
        out = deg[None, :, None] * (mi + b) + jnp.einsum('ij,bjo->bio', a, mj)
        return out

    def _L2_gnn_ref(h, adj, Wq, bq, Wk, bk, Wv, bv, Wo, bo):
        import jax, jax.numpy as jnp
        import numpy as np
        D_MODEL = 256
        NUM_HEADS = 8
        D_HEAD = D_MODEL // NUM_HEADS
        B, N = (4, 1024)
        b, n, _ = h.shape

        def split_heads(x):
            return x.reshape(b, n, NUM_HEADS, D_HEAD).transpose(0, 2, 1, 3)
        q = split_heads(h @ Wq.T + bq)
        k = split_heads(h @ Wk.T + bk)
        v = split_heads(h @ Wv.T + bv)
        scale = 1.0 / np.sqrt(D_HEAD)
        scores = jnp.einsum('bhqd,bhkd->bhqk', q, k) * scale
        mask = (adj == 0)[None, None, :, :]
        scores = jnp.where(mask, -jnp.inf, scores)
        attn = jax.nn.softmax(scores, axis=-1)
        out = jnp.einsum('bhqk,bhkd->bhqd', attn, v)
        out = out.transpose(0, 2, 1, 3).reshape(b, n, D_MODEL)
        return out @ Wo.T + bo

    def _L3_gnn_ref(x, adj, W, a_src, a_dst):
        import jax, jax.numpy as jnp
        import numpy as np
        B, N, D = (8, 1024, 256)
        NEG_SLOPE = 0.2
        Wh = jnp.einsum('bnd,de->bne', x, W)
        e_src = jnp.einsum('bnd,d->bn', Wh, a_src)
        e_dst = jnp.einsum('bnd,d->bn', Wh, a_dst)
        logits = e_src[:, :, None] + e_dst[:, None, :]
        logits = jnp.where(logits >= 0, logits, NEG_SLOPE * logits)
        mask = (adj == 0)[None, :, :]
        logits = jnp.where(mask, -jnp.inf, logits)
        attn = jax.nn.softmax(logits, axis=-1)
        attn = jnp.nan_to_num(attn, nan=0.0)
        out = jnp.einsum('bnm,bmd->bnd', attn, Wh)
        return out
    h = jnp.maximum(_layernorm(x, axis=-1), 0.0)
    x = x + _L0_gnn_ref(h, adj, L0_gnn_W, L0_gnn_a)
    h = jnp.maximum(_layernorm(x, axis=-1), 0.0)
    x = x + _L1_gnn_ref(h, adj, L1_gnn_W, L1_gnn_b)
    h = jnp.maximum(_layernorm(x, axis=-1), 0.0)
    x = x + _L2_gnn_ref(h, adj, L2_gnn_Wq, L2_gnn_bq, L2_gnn_Wk, L2_gnn_bk, L2_gnn_Wv, L2_gnn_bv, L2_gnn_Wo, L2_gnn_bo)
    h = jnp.maximum(_layernorm(x, axis=-1), 0.0)
    x = x + _L3_gnn_ref(h, adj, L3_gnn_W, L3_gnn_a_src, L3_gnn_a_dst)
    return x

_drawn_inputs = setup_inputs


def setup_inputs(seed=0):
    import zlib

    import numpy as np

    out = dict(_drawn_inputs(seed))
    spreads = {}
    factors = {'L2_gnn_Wq': 8.0,
     'L2_gnn_bq': 64.0,
     'L2_gnn_Wk': 8.0,
     'L2_gnn_bk': 64.0,
     'L2_gnn_bv': 8.0,
     'L2_gnn_bo': 7.185,
     'L3_gnn_a_src': 27.448,
     'L3_gnn_a_dst': 5.363}
    for name, (base, spread) in spreads.items():
        noise = np.random.default_rng([zlib.crc32(name.encode()), seed]).standard_normal(out[name].shape)
        drawn = base * np.exp(spread * noise) if base else spread * noise
        out[name] = jnp.asarray(drawn.astype(out[name].dtype))
    for name, factor in factors.items():
        out[name] = (out[name] * factor).astype(out[name].dtype)
    return out
```

```python
from contextlib import ExitStack

import concourse.bass as bass
from concourse import mybir

F32 = mybir.dt.float32
F16 = mybir.dt.float16
BF16 = mybir.dt.bfloat16
ALU = mybir.AluOpType
ACT = mybir.ActivationFunctionType
AX = mybir.AxisListType

P = 128
D = 256
KC = D // P
GROUP = 2
STREAMS = 4
HEADS = 8
DH = D // HEADS
QUADS = P // DH
BANKS = 2
BANK = 512
EPS = 1e-5
SLOPE = 0.2
MASKED = -1e30
WEIGHT_SCALE = 256.0
UNSCALE = 1.0 / WEIGHT_SCALE
F0 = 128
LAYERS = 4

COL_W0, COL_W3 = 0, F0 + 2
COL_WI = COL_W3 + D + 2
COL_WJ, COL_WQ, COL_WK, COL_WV, COL_WO = (COL_WI + D * k for k in range(1, 6))
COLS = COL_WO + D




def gat(l):
    return [f"stats{l}", f"rsqrt{l}", f"apply{l}", f"split{l}", f"split_lo{l}", f"turn{l}", f"turn{l}_copy",
            f"features{l}", f"features{l}_copy", f"features{l}_split", f"rows{l}", f"logits{l}", f"exp{l}",
            f"split_probs{l}", f"turn_probs{l}", f"turn_probs{l}_copy", f"sum{l}", f"residual{l}"]


def heads(p):
    return [f"scores_{p}", f"max_{p}", f"exp_{p}", f"split_heads_{p}", f"turn_heads_{p}", f"turn_heads_{p}_copy",
            f"sum_heads_{p}", f"normalise_{p}"]


PHASES = gat(0) + [
    "stats1", "rsqrt1", "apply1", "split1", "split_lo1", "bias1", "aggregate", "aggregate_copy", "aggregate_split",
    "messages", "residual1",
    "stats2", "rsqrt2", "apply2", "split2", "split_lo2", "bias2", "turn2", "turn2_copy", "query_key", "query_key_copy",
    "query_key_split", "values", "values_copy", "values_split"] + heads("a") + heads("b") + [
    "split_out", "split_out_lo", "turn_out", "turn_out_copy", "project", "residual2"] + gat(3) + ["store"]
PARTS = [PHASES[len(PHASES) * k // STREAMS:len(PHASES) * (k + 1) // STREAMS] for k in range(STREAMS)]


VECTOR_STEPS = [0, 10, 13, 16 + GROUP, 26 + GROUP]
SPLIT = {"h0": 0, "probs0": 1, "h1": 2, "h2": 3, "qk": 4, "heads": 8, "out": 8 + BANKS * GROUP,
         "h3": 9 + BANKS * GROUP, "probs3": 10 + BANKS * GROUP}
SPLITS = 11 + BANKS * GROUP
PSUM_SPLIT = {"features0": 0, "aggregates": 1, "values": 1 + GROUP, "features3": 2 + GROUP}
FROM_PSUM = 3 + GROUP
TURN = {"h0": 0, "probs0": 1, "h2": 2, "heads": 3, "out": 3 + GROUP, "h3": 4 + GROUP, "probs3": 5 + GROUP}
TURNS = 6 + GROUP


def beside(parts):
    at = [((k + 0.5) / len(part), s, name, i) for s, part, i in parts for k, name in enumerate(part)]
    return [(name, s, i) for _, s, name, i in sorted(at, key=lambda e: e[:2])]


def build(nc, x, adj, adj_t, w0, w0_t, a0, w_i, w_j, b1, w_q, w_k, b_qk, w_v, b_v, w_o, b_o, w3, w3_t, a3, out):
    graphs = x.shape[0]
    steps = graphs // (GROUP * STREAMS)
    assert graphs == steps * GROUP * STREAMS and x.shape[1] == P and x.shape[2] == D
    x_groups = x.rearrange("(g b) n d -> g n b d", b=GROUP)
    out_groups = out.rearrange("(g b) n d -> g n b d", b=GROUP)

    ctx = ExitStack()
    with ctx:
        def sb(name, shape, dt):
            return ctx.enter_context(nc.sbuf_tensor(name, shape, dt))

        def sem(name):
            return ctx.enter_context(nc.semaphore(name))

        def per_stream(name, shape, dt):
            return [sb(f"{name}{s}", shape, dt) for s in range(STREAMS)]

        adj_i = sb("adj_i", [P, 2, P], mybir.dt.int32)
        adj_f = sb("adj_f", [P, 2, P], F32)
        degree = sb("degree", [P, 1], F32)
        mask = sb("mask", [P, 2, P], BF16)
        agg_deg = sb("agg_deg", [P, 2 * P], F16)
        ident = sb("ident", [P, P], F32)
        ident_h = sb("ident_h", [P, P], F16)
        ident_b = sb("ident_b", [P, P], BF16)
        ones_h = sb("ones_h", [P, P], F16)
        minus_half = sb("minus_half", [P, GROUP], F32)
        w_f = sb("w_f", [P, KC, COLS], F32)
        w_hi = sb("w_hi", [P, KC, COLS], F16)
        w_lo = sb("w_lo", [P, KC, COLS], F16)
        w0t_f = sb("w0t_f", [P, D], F32)
        w3t_f = sb("w3t_f", [P, KC, D], F32)
        a0_f = sb("a0_f", [P, 2], F32)
        a3_f = sb("a3_f", [P, KC, 2], F32)
        bqk = sb("bqk", [P, 2 * KC], F32)
        bv_col = sb("bv_col", [P, KC], F32)
        bv_wide = sb("bv_wide", [P, KC, P], F32)
        b1_row = sb("b1_row", [P, D], F32)
        bo_row = sb("bo_row", [P, D], F32)
        bias1 = sb("bias1", [P, D], F32)
        bias2 = sb("bias2", [P, D], F32)

        x_in = per_stream("x_in", [P, GROUP, D], F32)
        xs = per_stream("xs", [P, GROUP, D], F32)
        y = per_stream("y", [P, GROUP, D], F32)
        stats = per_stream("stats", [P, GROUP, 6], F32)
        mean2 = per_stream("mean2", [P, GROUP], F32)
        var = per_stream("var", [P, GROUP], F32)
        m2 = per_stream("m2", [P, GROUP], F32)
        gap = per_stream("gap", [P, GROUP], F32)
        rstd = per_stream("rstd", [P, GROUP], F32)
        shift = per_stream("shift", [P, GROUP], F32)
        nat = per_stream("nat", [P, GROUP, D], F32)
        nat_hi = per_stream("nat_hi", [P, GROUP, D], F16)
        nat_lo = per_stream("nat_lo", [P, GROUP, D], F16)
        turned = per_stream("turned", [P, 2, KC, GROUP * P], F16)
        g_hi = [per_stream("g0_hi", [P, GROUP, F0 + 1], F16), per_stream("g3_hi", [P, GROUP, D + 1], F16)]
        g_lo = [per_stream("g0_lo", [P, GROUP, F0 + 1], F16), per_stream("g3_lo", [P, GROUP, D + 1], F16)]
        src_dst = per_stream("src_dst", [P, GROUP, 2], F32)
        dst_h = per_stream("dst_h", [P, 2, GROUP], F16)
        dst_diag = per_stream("dst_diag", [P, 2, GROUP, P], F16)
        za = per_stream("za", [P, GROUP, P], F32)
        zb = per_stream("zb", [P, GROUP, P], F32)
        gmax = per_stream("gmax", [P, GROUP], F32)
        grec = per_stream("grec", [P, GROUP], F32)
        wide = per_stream("wide", [P, 2 * KC, GROUP * P], F32)
        wide_hi = per_stream("wide_hi", [P, 2 * KC, GROUP * P], F16)
        wide_lo = per_stream("wide_lo", [P, 2 * KC, GROUP * P], F16)
        agg_h, agg_l = ([t[:, :, :].rearrange("p (b k) n -> p b (k n)", b=GROUP) for t in w] for w in (wide_hi, wide_lo))
        prob = per_stream("prob", [P, BANKS, BANK], F32)
        prob_hi = per_stream("prob_hi", [P, BANKS, BANK], F16)
        prob_lo = per_stream("prob_lo", [P, BANKS, BANK], F16)
        prob_t = per_stream("prob_t", [P, BANKS, 2, BANK], F16)
        v_hi = per_stream("v_hi", [P, GROUP, HEADS, DH + 1], F16)
        v_lo = per_stream("v_lo", [P, GROUP, HEADS, DH + 1], F16)
        hmax = per_stream("hmax", [P, BANKS, HEADS // BANKS], F32)
        hrec = per_stream("hrec", [P, HEADS], F32)

        ps = [ctx.enter_context(nc.psum_tensor(f"ps{s}", [P, BANKS, BANK], F32)) for s in range(STREAMS)]
        ps_h = [ps[s][:, :, :].bitcast(F16) for s in range(STREAMS)]

        def qk_out(s, j):
            return ps[s][:, j // KC, (j % KC) * GROUP * P:(j % KC + 1) * GROUP * P]

        loads = sem("constants_loaded")
        ident_ready = sem("ident_ready")
        setup = sem("setup_steps")
        setup_pe = sem("setup_products")
        const_done = sem("constants_ready")

        class Signal:

            def __init__(self, name, per_step):
                self.sem = [sem(f"{name}{s}") for s in range(STREAMS)]
                self.per_step = per_step

            def __getitem__(self, s):
                return self.sem[s]

            def at(self, i, k):
                return i * self.per_step + k

        loaded = Signal("loaded", 16)
        stored = Signal("stored", 16)
        steps_done = Signal("vector_steps", VECTOR_STEPS[LAYERS])
        moments = Signal("moments", LAYERS)
        norm_scale = Signal("norm_scale", LAYERS)
        norm_ready = Signal("norm_ready", LAYERS)
        full = Signal("full", SPLITS)
        hi_part = Signal("hi_part", SPLITS)
        lo_part = Signal("lo_part", SPLITS)
        psum_hi = Signal("psum_hi", FROM_PSUM)
        psum_lo = Signal("psum_lo", FROM_PSUM)
        turned_a = Signal("turned_a", TURNS)
        turned_b = Signal("turned_b", TURNS)
        copied_a = Signal("copied_a", TURNS)
        copied_b = Signal("copied_b", TURNS)
        x_updated = Signal("x_updated", LAYERS)
        bias_added = Signal("bias_added", 2)
        g_made = Signal("gat_features", 2)
        diag_hi = Signal("diag_hi", 2)
        diag_lo = Signal("diag_lo", 2)
        dst_rows = Signal("dst_rows", 2)
        logits = Signal("logits", 2)
        g_out = Signal("gat_out", 2)
        agg = Signal("aggregated", GROUP)
        update = Signal("update", 2 * GROUP)
        qk = Signal("query_key", 2 * KC)
        v_made = Signal("values", GROUP)
        scores = Signal("scores", GROUP)
        half_scores = Signal("half_scores", GROUP)
        row_max = Signal("row_max", BANKS * GROUP)
        heads_out = Signal("heads_out", GROUP)
        bank_free = Signal("bank_free", GROUP - 1)

        both = range(STREAMS)

        def run(eng, phases):
            def slots(i, first=False, last=False):
                for r in range(STREAMS):
                    now = [(s, PARTS[(r - s) % STREAMS], i if s <= r else i - 1) for s in range(STREAMS)
                           if not (first and s > r) and not (last and s <= r)]
                    for name, s, step in beside(now):
                        if name in phases:
                            phases[name](step, s)

            slots(0, first=True)
            with eng.Fori(1, steps) as i:
                slots(i)
            slots(steps, last=True)

        block = ctx.enter_context(nc.Block())

        @block.sync
        def _(sp):
            for dst, src in (
                (adj_i[:, 0, :], adj), (adj_i[:, 1, :], adj_t),
                (w_f[:, :, COL_W0:COL_W0 + F0], w0.rearrange("(c p) n -> p c n", p=P)),
                (w_f[:, :, COL_W3:COL_W3 + D], w3.rearrange("(c p) n -> p c n", p=P)),
                (w_f[:, :, COL_WI:COL_WI + D], w_i.rearrange("(c p) n -> p c n", p=P)),
                (w_f[:, :, COL_WJ:COL_WJ + D], w_j.rearrange("(c p) n -> p c n", p=P)),
                (w_f[:, :, COL_WQ:COL_WQ + D], w_q.rearrange("(c p) n -> p c n", p=P)),
                (w_f[:, :, COL_WK:COL_WK + D], w_k.rearrange("(c p) n -> p c n", p=P)),
                (w_f[:, :, COL_WV:COL_WV + D], w_v.rearrange("(c p) n -> p c n", p=P)),
                (w_f[:, :, COL_WO:COL_WO + D], w_o.rearrange("(c p) n -> p c n", p=P)),
                (w0t_f[:, :], w0_t), (w3t_f[:, :, :], w3_t.rearrange("(c p) n -> p c n", p=P)),
                (a0_f[:, :], a0), (a3_f[:, :, :], a3.rearrange("(c p) k -> p c k", p=P)),
                (bqk[:, :], b_qk), (bv_col[:, :], b_v),
                (b1_row[:, :], b1.partition_broadcast(P)), (bo_row[:, :], b_o.partition_broadcast(P)),
            ):
                sp.dma_start(dst, src).then_inc(loads, 16)
            for s in both:
                sp.dma_start(x_in[s][:, :, :], x_groups[s]).then_inc(loaded[s], 16)
            with sp.Fori(1, steps) as i:
                for s in both:
                    sp.wait_ge(x_updated[s], x_updated.at(i - 1, 1))
                    sp.dma_start(x_in[s][:, :, :], x_groups[i * STREAMS + s]).then_inc(loaded[s], 16)
            for s in both:
                sp.wait_ge(stored[s], 16 + stored.at(steps - 1, 16))

        n_loads = 18 * 16

        @block.tensor
        def _(pe):
            pe.wait_ge(loads, n_loads)
            pe.wait_ge(setup, 2)
            for c in range(KC):
                pe.matmul(ps[0][:, 0, 2 * c:2 * c + 2], w0t_f[:, c * P:(c + 1) * P], a0_f[:, :], start=True, stop=True)
            for c in range(KC):
                for e in range(KC):
                    pe.matmul(ps[0][:, 1, 2 * c:2 * c + 2], w3t_f[:, e, c * P:(c + 1) * P], a3_f[:, e, :],
                              start=(e == 0), stop=(e == KC - 1))
            for c in range(KC):
                last = pe.matmul(ps[1][:, 0, 0:D], bv_wide[:, c, :], w_f[:, c, COL_WO:COL_WO + D],
                                 start=(c == 0), stop=(c == KC - 1))
            last.then_inc(setup_pe, 1)
            pe.wait_ge(const_done, 1)

            def product(out_ap, left, right, c0=0):
                for c in range(KC):
                    (lh, ll), (rh, rl) = left(c), right(c)
                    pe.matmul(out_ap, lh, rh, start=(c0 + c == 0), stop=False)
                    pe.matmul(out_ap, lh, rl, start=False, stop=False)
                    last = pe.matmul(out_ap, ll, rh, start=False, stop=(c == KC - 1))
                return last

            def weights(col, n):
                return lambda c: (w_hi[:, c, col:col + n], w_lo[:, c, col:col + n])

            def turned_cols(s, b, n):
                return lambda c: (turned[s][:, 0, c, b * P:b * P + n], turned[s][:, 1, c, b * P:b * P + n])

            def turn(i, s, what):
                for bank, (part, src, done) in enumerate(((hi_part, nat_hi, turned_a), (lo_part, nat_lo, turned_b))):
                    pe.wait_ge(part[s], part.at(i, SPLIT[what] + 1))
                    for c in range(KC):
                        for b in range(GROUP):
                            last = pe.transpose(ps_h[s][:, bank, (c * GROUP + b) * P:(c * GROUP + b + 1) * P],
                                                src[s][:, b, c * P:(c + 1) * P], ident_h[:, :])
                    last.then_inc(done[s], 1)

            def wait_turned(i, s, what):
                pe.wait_ge(copied_a[s], copied_a.at(i, TURN[what] + 1))
                pe.wait_ge(copied_b[s], copied_b.at(i, TURN[what] + 1))

            def gat_features(i, s, a):
                f, col = (F0, COL_W0) if a == 0 else (D, COL_W3)
                wait_turned(i, s, ("h0", "h3")[a])
                for b in range(GROUP):
                    last = product(ps[s][:, b, 0:f + 2], turned_cols(s, b, P), weights(col, f + 2))
                last.then_inc(g_made[s], 1)

            def gat_dst_rows(i, s, a):
                pe.wait_ge(psum_lo[s], psum_lo.at(i, PSUM_SPLIT[("features0", "features3")[a]] + 1))
                pe.wait_ge(steps_done[s], steps_done.at(i, VECTOR_STEPS[3 * a] + 4))
                pe.wait_ge(diag_hi[s], diag_hi.at(i, a + 1))
                pe.matmul(ps[s][:, 0, 0:GROUP * P], ident_b[:, :], mask[:, :, :].rearrange("p g j -> p (g j)"), start=True, stop=False)
                pe.matmul(ps[s][:, 0, 0:GROUP * P], ones_h[:, :], dst_diag[s][:, 0, :, :].rearrange("p g j -> p (g j)"),
                          start=False, stop=False)
                pe.wait_ge(diag_lo[s], diag_lo.at(i, a + 1))
                pe.matmul(ps[s][:, 0, 0:GROUP * P], ones_h[:, :], dst_diag[s][:, 1, :, :].rearrange("p g j -> p (g j)"),
                          start=False, stop=True).then_inc(dst_rows[s], 1)

            def gat_turn(i, s, a):
                k = SPLIT[("probs0", "probs3")[a]]
                for bank, (part, src, done) in ((1, (hi_part, prob_hi, turned_a)), (0, (lo_part, prob_lo, turned_b))):
                    pe.wait_ge(part[s], part.at(i, k + 1))
                    for b in range(GROUP):
                        last = pe.transpose(ps_h[s][:, bank, b * P:(b + 1) * P], src[s][:, 0, b * P:(b + 1) * P], ident_h[:, :])
                    last.then_inc(done[s], 1)

            def gat_sum(i, s, a):
                f = F0 if a == 0 else D
                wait_turned(i, s, ("probs0", "probs3")[a])
                for b in range(GROUP):
                    ph, pl = (prob_t[s][:, 0, k, b * P:(b + 1) * P] for k in range(2))
                    o = ps[s][:, b, 0:f + 1]
                    pe.matmul(o, ph, g_hi[a][s][:, b, :], start=True, stop=False)
                    pe.matmul(o, ph, g_lo[a][s][:, b, :], start=False, stop=False)
                    last = pe.matmul(o, pl, g_hi[a][s][:, b, :], start=False, stop=True)
                last.then_inc(g_out[s], 1)

            def aggregate(i, s):
                pe.wait_ge(hi_part[s], hi_part.at(i, SPLIT["h1"] + 1))
                pe.wait_ge(lo_part[s], lo_part.at(i, SPLIT["h1"] + 1))
                for b in range(GROUP):
                    for c in range(KC):
                        o = ps[s][:, b, c * 2 * P:(c + 1) * 2 * P]
                        pe.matmul(o, nat_hi[s][:, b, c * P:(c + 1) * P], agg_deg[:, :], start=True, stop=False)
                        last = pe.matmul(o, nat_lo[s][:, b, c * P:(c + 1) * P], agg_deg[:, :], start=False, stop=True)
                    last.then_inc(agg[s], 1)

            def messages(i, s):
                for b in range(GROUP):
                    pe.wait_ge(psum_hi[s], psum_hi.at(i, PSUM_SPLIT["aggregates"] + b + 1))
                    pe.wait_ge(psum_lo[s], psum_lo.at(i, PSUM_SPLIT["aggregates"] + b + 1))
                    for part, col in ((0, COL_WJ), (1, COL_WI)):
                        at = lambda c: slice(c * 2 * P + part * P, c * 2 * P + (part + 1) * P)
                        o = ps[s][:, b, 0:D]
                        for c in range(KC):
                            lh, ll = agg_h[s][:, b, at(c)], agg_l[s][:, b, at(c)]
                            rh, rl = weights(col, D)(c)
                            pe.matmul(o, lh, rh, start=(part == 0 and c == 0), stop=False)
                            pe.matmul(o, lh, rl, start=False, stop=False)
                            last = pe.matmul(o, ll, rh, start=False, stop=(part == 1 and c == KC - 1))
                    last.then_inc(update[s], 1)

            def query_key(i, s):
                wait_turned(i, s, "h2")
                for j in range(4):
                    col = (COL_WQ, COL_WK)[j // KC] + (j % KC) * P
                    product(qk_out(s, j), weights(col, P), turned_cols(s, 0, GROUP * P)).then_inc(qk[s], 1)

            def values(i, s):
                for b in range(GROUP):
                    pe.wait_ge(full[s], full.at(i, SPLIT["qk"] + KC * (b + 1)))
                    product(ps[s][:, b, 0:D], turned_cols(s, b, P), weights(COL_WV, D)).then_inc(v_made[s], 1)

            def head_scores(i, s, b):
                if b == 0:
                    pe.wait_ge(hi_part[s], hi_part.at(i, SPLIT["qk"] + 2 * KC))
                    pe.wait_ge(lo_part[s], lo_part.at(i, SPLIT["qk"] + 2 * KC))
                    pe.wait_ge(psum_hi[s], psum_hi.at(i, PSUM_SPLIT["values"] + 1))
                    pe.wait_ge(psum_lo[s], psum_lo.at(i, PSUM_SPLIT["values"] + 1))
                else:
                    pe.wait_ge(bank_free[s], bank_free.at(i, b))
                for half in range(2):
                    for k in range(BANKS):
                        pe.matmul(ps[s][:, k, half * KC * P:(half + 1) * KC * P], ident_b[:, :],
                                  mask[:, :, :].rearrange("p g j -> p (g j)"), start=True, stop=False)
                    if half == 1:
                        pe.wait_ge(half_scores[s], half_scores.at(i, b + 1))
                    for c in range(KC):
                        for t, (q, kk) in enumerate(((wide_hi, wide_hi), (wide_hi, wide_lo), (wide_lo, wide_hi))):
                            for k in range(BANKS):
                                a = half * BANKS + k
                                rows = slice(a * DH, (a + 1) * DH)
                                last = pe.matmul(ps[s][:, k, (half * KC + c) * P:(half * KC + c + 1) * P],
                                                 q[s][rows, c, b * P:(b + 1) * P], kk[s][rows, KC + c, b * P:(b + 1) * P],
                                                 start=False, stop=(t == 2 and c == KC - 1))
                    last.then_inc((half_scores, scores)[half][s], 1)

            def head_turn(i, s, b):
                for k, done in enumerate((turned_a, turned_b)):
                    pe.wait_ge(hi_part[s], hi_part.at(i, SPLIT["heads"] + BANKS * b + k + 1))
                    pe.wait_ge(lo_part[s], lo_part.at(i, SPLIT["heads"] + BANKS * b + k + 1))
                    for part, src in enumerate((prob_hi, prob_lo)):
                        for j in range(BANK // P):
                            last = pe.transpose(ps_h[s][:, k, part * BANK + j * P:part * BANK + (j + 1) * P],
                                                src[s][:, k, j * P:(j + 1) * P], ident_h[:, :])
                    last.then_inc(done[s], 1)

            def head_sum(i, s, b):
                pe.wait_ge(copied_a[s], copied_a.at(i, TURN["heads"] + b + 1))
                pe.wait_ge(copied_b[s], copied_b.at(i, TURN["heads"] + b + 1))
                for h in range(HEADS):
                    c, a = h // QUADS, h % QUADS
                    o = ps[s][:, 0, h * (DH + 1):(h + 1) * (DH + 1)]
                    col = ((a // BANKS) * KC + c) * P
                    ph, pl = (prob_t[s][:, a % BANKS, part, col:col + P] for part in range(2))
                    pe.matmul(o, ph, v_hi[s][:, b, h, :], start=True, stop=False)
                    pe.matmul(o, ph, v_lo[s][:, b, h, :], start=False, stop=False)
                    last = pe.matmul(o, pl, v_hi[s][:, b, h, :], start=False, stop=True)
                last.then_inc(heads_out[s], 1)

            def project(i, s):
                wait_turned(i, s, "out")
                for b in range(GROUP):
                    product(ps[s][:, b, 0:D], turned_cols(s, b, P), weights(COL_WO, D)).then_inc(update[s], 1)

            run(pe, {
                "turn0": lambda i, s: turn(i, s, "h0"), "features0": lambda i, s: gat_features(i, s, 0),
                "rows0": lambda i, s: gat_dst_rows(i, s, 0), "turn_probs0": lambda i, s: gat_turn(i, s, 0),
                "sum0": lambda i, s: gat_sum(i, s, 0),
                "aggregate": aggregate, "messages": messages,
                "turn2": lambda i, s: turn(i, s, "h2"), "query_key": query_key, "values": values,
                "scores_a": lambda i, s: head_scores(i, s, 0), "turn_heads_a": lambda i, s: head_turn(i, s, 0),
                "sum_heads_a": lambda i, s: head_sum(i, s, 0),
                "scores_b": lambda i, s: head_scores(i, s, 1), "turn_heads_b": lambda i, s: head_turn(i, s, 1),
                "sum_heads_b": lambda i, s: head_sum(i, s, 1),
                "turn_out": lambda i, s: turn(i, s, "out"), "project": project,
                "turn3": lambda i, s: turn(i, s, "h3"), "features3": lambda i, s: gat_features(i, s, 1),
                "rows3": lambda i, s: gat_dst_rows(i, s, 1), "turn_probs3": lambda i, s: gat_turn(i, s, 1),
                "sum3": lambda i, s: gat_sum(i, s, 1),
            })

        @block.vector
        def _(dve):
            dve.wait_ge(loads, n_loads)
            n = 0

            def link(ins):
                nonlocal n
                ins.then_inc(setup, 1)
                n += 1
                dve.wait_ge(setup, n)

            for s in both:
                dve.memset(y[s][:, :, :], 0.0).then_inc(stored[s], 16)
            link(dve.memset(bv_wide[:, :, :], 0.0))
            for c in range(KC):
                last = dve.tensor_scalar(bv_wide[:, c, :], bv_wide[:, c, :], bv_col[:, c:c + 1], None, ALU.add)
            link(last)
            link(dve.tensor_copy(adj_f[:, :, :], adj_i[:, :, :]))
            dve.tensor_copy(agg_deg[:, 0:P], adj_f[:, 1, :])
            for g in range(2):
                dve.tensor_scalar(mask[:, g, :], adj_f[:, 0, :], -1.0, -MASKED, ALU.add, ALU.mult)
            link(dve.tensor_reduce(degree[:, :], adj_f[:, 0, :], AX.X, ALU.add))
            dve.tensor_scalar(bias1[:, :], b1_row[:, :], degree[:, 0:1], None, ALU.mult)
            dve.memset(minus_half[:, :], -0.5)
            dve.memset(ones_h[:, :], 1.0)
            for s in both:
                dve.memset(g_hi[0][s][:, :, F0:F0 + 1], 1.0)
                dve.memset(g_hi[1][s][:, :, D:D + 1], 1.0)
                dve.memset(g_lo[0][s][:, :, F0:F0 + 1], 0.0)
                dve.memset(g_lo[1][s][:, :, D:D + 1], 0.0)
                dve.memset(v_hi[s][:, :, :, DH:DH + 1], 1.0)
                dve.memset(v_lo[s][:, :, :, DH:DH + 1], 0.0)
            dve.tensor_scalar(bqk[:, 0:KC], bqk[:, 0:KC], float(DH) ** -0.5, None, ALU.mult)
            dve.wait_ge(setup_pe, 1)
            dve.tensor_copy(w_f[:, :, COL_W0 + F0:COL_W0 + F0 + 2], ps[0][:, 0, 0:2 * KC].rearrange("p (c k) -> p c k", c=KC))
            dve.tensor_copy(w_f[:, :, COL_W3 + D:COL_W3 + D + 2], ps[0][:, 1, 0:2 * KC].rearrange("p (c k) -> p c k", c=KC))
            link(dve.tensor_tensor(bias2[:, :], ps[1][:, 0, 0:D], bo_row[:, :], ALU.add))
            link(dve.tensor_scalar(w_f[:, :, :], w_f[:, :, :], WEIGHT_SCALE, None, ALU.mult))
            link(dve.tensor_copy(w_hi[:, :, :], w_f[:, :, :]))
            dve.tensor_tensor(w_lo[:, :, :], w_f[:, :, :], w_hi[:, :, :], ALU.subtract)
            dve.wait_ge(ident_ready, 2)
            dve.tensor_copy(ident_h[:, :], ident[:, :])
            dve.tensor_copy(ident_b[:, :], ident[:, :])
            dve.tensor_scalar(agg_deg[:, P:2 * P], ident[:, :], degree[:, 0:1], None, ALU.mult).then_inc(const_done, 1)
            dve.wait_ge(const_done, 1)

            def src(l, s):
                return (x_in if l == 0 else xs)[s]

            def norm_stats(i, s, l):
                if l == 0:
                    dve.wait_ge(loaded[s], loaded.at(i, 16))
                else:
                    dve.wait_ge(x_updated[s], x_updated.at(i, l))
                for b in range(GROUP):
                    last = dve.bn_stats(stats[s][:, b, :], src(l, s)[:, b, :])
                last.then_inc(steps_done[s], 1)
                dve.wait_ge(steps_done[s], steps_done.at(i, VECTOR_STEPS[l] + 1))
                even, odd = stats[s][:, :, 0:3], stats[s][:, :, 3:6]
                dve.tensor_tensor(gap[s][:, :], even[:, :, 1], odd[:, :, 1], ALU.subtract)
                dve.tensor_tensor(mean2[s][:, :], even[:, :, 1], odd[:, :, 1], ALU.add)
                dve.tensor_tensor(m2[s][:, :], even[:, :, 2], odd[:, :, 2], ALU.add).then_inc(steps_done[s], 1)
                dve.wait_ge(steps_done[s], steps_done.at(i, VECTOR_STEPS[l] + 2))
                dve.scalar_tensor_tensor(gap[s][:, :], gap[s][:, :], 0.25, gap[s][:, :], ALU.mult, ALU.mult)
                dve.tensor_scalar(m2[s][:, :], m2[s][:, :], 1.0 / D, EPS, ALU.mult, ALU.add)
                dve.tensor_scalar(mean2[s][:, :], mean2[s][:, :], -0.5, None, ALU.mult).then_inc(steps_done[s], 1)
                dve.wait_ge(steps_done[s], steps_done.at(i, VECTOR_STEPS[l] + 3))
                dve.tensor_tensor(var[s][:, :], m2[s][:, :], gap[s][:, :], ALU.add).then_inc(moments[s], 1)

            def split_hi(i, s, what):
                dve.wait_ge(full[s], full.at(i, SPLIT[what] + 1))
                dve.tensor_copy(nat_hi[s][:, :, :], nat[s][:, :, :]).then_inc(hi_part[s], 1)

            def copy_turned_hi(i, s, what):
                dve.wait_ge(turned_a[s], turned_a.at(i, TURN[what] + 1))
                dve.tensor_copy(turned[s][:, 0, :, :].rearrange("p c n -> p (c n)"), ps_h[s][:, 0, 0:KC * GROUP * P])\
                   .then_inc(copied_a[s], 1)

            def gat_split(i, s, a):
                f = F0 if a == 0 else D
                dve.wait_ge(g_made[s], g_made.at(i, a + 1))
                dve.wait_ge(psum_hi[s], psum_hi.at(i, PSUM_SPLIT[("features0", "features3")[a]] + 1))
                dve.tensor_scalar(src_dst[s][:, :, :], ps[s][:, :, f:f + 2], UNSCALE, None, ALU.mult).then_inc(steps_done[s], 1)
                dve.wait_ge(steps_done[s], steps_done.at(i, VECTOR_STEPS[3 * a] + 4))
                dve.tensor_copy(dst_h[s][:, 0, :], src_dst[s][:, :, 1]).then_inc(steps_done[s], 1)
                dve.wait_ge(steps_done[s], steps_done.at(i, VECTOR_STEPS[3 * a] + 5))
                dve.tensor_tensor(dst_h[s][:, 1, :], src_dst[s][:, :, 1], dst_h[s][:, 0, :], ALU.subtract).then_inc(steps_done[s], 1)
                dve.tensor_tensor(dst_diag[s][:, 0, :, :], ident_h[:, :].unsqueeze(1).to_broadcast([P, GROUP, P]),
                                  dst_h[s][:, 0, :].unsqueeze(2).to_broadcast([P, GROUP, P]), ALU.mult).then_inc(diag_hi[s], 1)
                last = dve.scalar_tensor_tensor(g_lo[a][s][:, :, 0:f], ps[s][:, :, 0:f], UNSCALE, g_hi[a][s][:, :, 0:f],
                                                ALU.mult, ALU.subtract)
                if a == 0:
                    last = dve.scalar_tensor_tensor(xs[s][:, :, F0:D], ps[s][:, :, 0:F0], UNSCALE, x_in[s][:, :, F0:D],
                                                    ALU.mult, ALU.add)
                last.then_inc(psum_lo[s], 1)

            def gat_logits(i, s, a):
                dve.wait_ge(dst_rows[s], dst_rows.at(i, a + 1))
                dve.tensor_tensor(za[s][:, :, :], ps[s][:, 0, 0:GROUP * P].rearrange("p (g j) -> p g j", g=GROUP),
                                  src_dst[s][:, :, 0:1].to_broadcast([P, GROUP, P]), ALU.add).then_inc(steps_done[s], 1)
                dve.wait_ge(steps_done[s], steps_done.at(i, VECTOR_STEPS[3 * a] + 7))
                dve.scalar_tensor_tensor(zb[s][:, :, :], za[s][:, :, :], SLOPE, za[s][:, :, :], ALU.mult, ALU.max)\
                   .then_inc(steps_done[s], 1)
                dve.wait_ge(steps_done[s], steps_done.at(i, VECTOR_STEPS[3 * a] + 8))
                dve.tensor_reduce(gmax[s][:, :], zb[s][:, :, :], AX.X, ALU.max).then_inc(steps_done[s], 1)
                dve.wait_ge(steps_done[s], steps_done.at(i, VECTOR_STEPS[3 * a] + 9))
                dve.tensor_tensor(za[s][:, :, :], zb[s][:, :, :], gmax[s][:, :].unsqueeze(2).to_broadcast([P, GROUP, P]),
                                  ALU.subtract).then_inc(logits[s], 1)

            def gat_prob_split(i, s, a):
                dve.wait_ge(full[s], full.at(i, SPLIT[("probs0", "probs3")[a]] + 1))
                dve.tensor_copy(prob_hi[s][:, 0, 0:GROUP * P], prob[s][:, 0, 0:GROUP * P]).then_inc(hi_part[s], 1)

            def gat_copy_prob_t(i, s, a):
                dve.wait_ge(turned_a[s], turned_a.at(i, TURN[("probs0", "probs3")[a]] + 1))
                dve.tensor_copy(prob_t[s][:, 0, 0, 0:GROUP * P], ps_h[s][:, 1, 0:GROUP * P]).then_inc(copied_a[s], 1)

            def gat_residual(i, s, a):
                f = F0 if a == 0 else D
                dve.wait_ge(g_out[s], g_out.at(i, a + 1))
                dve.reciprocal(grec[s][:, :], ps[s][:, :, f]).then_inc(steps_done[s], 1)
                dve.wait_ge(steps_done[s], steps_done.at(i, VECTOR_STEPS[3 * a] + 10))
                if a == 1:
                    dve.wait_ge(stored[s], 16 + stored.at(i, 0))
                old, new = ((x_in, xs) if a == 0 else (xs, y))
                for b in range(GROUP):
                    last = dve.scalar_tensor_tensor(new[s][:, b, 0:f], ps[s][:, b, 0:f], grec[s][:, b:b + 1], old[s][:, b, 0:f],
                                                    ALU.mult, ALU.add)
                last.then_inc(x_updated[s], 1)

            def agg_split(i, s):
                for b in range(GROUP):
                    dve.wait_ge(psum_hi[s], psum_hi.at(i, PSUM_SPLIT["aggregates"] + b + 1))
                    dve.tensor_tensor(agg_l[s][:, b, :], ps[s][:, b, :], agg_h[s][:, b, :], ALU.subtract).then_inc(psum_lo[s], 1)

            def messages_residual(i, s):
                dve.wait_ge(bias_added[s], bias_added.at(i, 1))
                dve.wait_ge(update[s], update.at(i, GROUP))
                dve.scalar_tensor_tensor(xs[s][:, :, :], ps[s][:, :, 0:D], UNSCALE, xs[s][:, :, :], ALU.mult, ALU.add)\
                   .then_inc(x_updated[s], 1)

            def qk_split(i, s):
                for j in range(4):
                    dve.wait_ge(full[s], full.at(i, SPLIT["qk"] + j + 1))
                    dve.tensor_copy(wide_hi[s][:, j, :], wide[s][:, j, :]).then_inc(hi_part[s], 1)

            def v_split(i, s):
                dve.wait_ge(psum_hi[s], psum_hi.at(i, PSUM_SPLIT["values"] + 1))
                for b in range(GROUP):
                    last = dve.scalar_tensor_tensor(v_lo[s][:, b, :, 0:DH], ps[s][:, b, 0:D].rearrange("p (h d) -> p h d", h=HEADS),
                                                    UNSCALE, v_hi[s][:, b, :, 0:DH], ALU.mult, ALU.subtract)
                last.then_inc(psum_lo[s], 1)

            def head_max(i, s, b):
                dve.wait_ge(scores[s], scores.at(i, b + 1))
                for k in range(BANKS):
                    dve.tensor_reduce(hmax[s][:, k, :], ps[s][:, k, :].rearrange("p (j k) -> p j k", k=P), AX.X, ALU.max,
                                      negate=True).then_inc(row_max[s], 1)

            def head_prob_split(i, s, b):
                for k in range(BANKS):
                    dve.wait_ge(full[s], full.at(i, SPLIT["heads"] + BANKS * b + k + 1))
                    dve.tensor_copy(prob_hi[s][:, k, :], prob[s][:, k, :]).then_inc(hi_part[s], 1)

            def head_copy_bank0(i, s, b):
                dve.wait_ge(turned_a[s], turned_a.at(i, TURN["heads"] + b + 1))
                dve.tensor_copy(prob_t[s][:, 0, :, :].rearrange("p k n -> p (k n)"), ps_h[s][:, 0, :]).then_inc(copied_a[s], 1)

            def head_normalise(i, s, b):
                dve.wait_ge(heads_out[s], heads_out.at(i, b + 1))
                o = ps[s][:, 0, 0:HEADS * (DH + 1)].rearrange("p (h d) -> p h d", h=HEADS)
                dve.reciprocal(hrec[s][:, :], o[:, :, DH]).then_inc(steps_done[s], 1)
                dve.wait_ge(steps_done[s], steps_done.at(i, VECTOR_STEPS[2] + 3 + b + 1))
                dve.tensor_tensor(nat[s][:, b, :].rearrange("p (h d) -> p h d", h=HEADS), o[:, :, 0:DH],
                                  hrec[s][:, :].unsqueeze(2).to_broadcast([P, HEADS, DH]), ALU.mult)\
                   .then_inc((full if b == GROUP - 1 else bank_free)[s], 1)

            def project_residual(i, s):
                dve.wait_ge(bias_added[s], bias_added.at(i, 2))
                dve.wait_ge(update[s], update.at(i, 2 * GROUP))
                dve.scalar_tensor_tensor(xs[s][:, :, :], ps[s][:, :, 0:D], UNSCALE, xs[s][:, :, :], ALU.mult, ALU.add)\
                   .then_inc(x_updated[s], 1)

            run(dve, {
                **{f"stats{l}": lambda i, s, l=l: norm_stats(i, s, l) for l in range(LAYERS)},
                **{f"split{l}": lambda i, s, l=l: split_hi(i, s, f"h{l}") for l in range(LAYERS)},
                "turn0_copy": lambda i, s: copy_turned_hi(i, s, "h0"), "turn2_copy": lambda i, s: copy_turned_hi(i, s, "h2"),
                "turn_out_copy": lambda i, s: copy_turned_hi(i, s, "out"), "turn3_copy": lambda i, s: copy_turned_hi(i, s, "h3"),
                "features0_split": lambda i, s: gat_split(i, s, 0), "features3_split": lambda i, s: gat_split(i, s, 1),
                "logits0": lambda i, s: gat_logits(i, s, 0), "logits3": lambda i, s: gat_logits(i, s, 1),
                "split_probs0": lambda i, s: gat_prob_split(i, s, 0), "split_probs3": lambda i, s: gat_prob_split(i, s, 1),
                "turn_probs0_copy": lambda i, s: gat_copy_prob_t(i, s, 0),
                "turn_probs3_copy": lambda i, s: gat_copy_prob_t(i, s, 1),
                "residual0": lambda i, s: gat_residual(i, s, 0), "residual3": lambda i, s: gat_residual(i, s, 1),
                "aggregate_split": agg_split, "residual1": messages_residual,
                "query_key_split": qk_split, "values_split": v_split,
                "max_a": lambda i, s: head_max(i, s, 0), "max_b": lambda i, s: head_max(i, s, 1),
                "split_heads_a": lambda i, s: head_prob_split(i, s, 0), "split_heads_b": lambda i, s: head_prob_split(i, s, 1),
                "turn_heads_a_copy": lambda i, s: head_copy_bank0(i, s, 0),
                "turn_heads_b_copy": lambda i, s: head_copy_bank0(i, s, 1),
                "normalise_a": lambda i, s: head_normalise(i, s, 0), "normalise_b": lambda i, s: head_normalise(i, s, 1),
                "split_out": lambda i, s: split_hi(i, s, "out"), "residual2": project_residual,
            })

        @block.scalar
        def _(act):
            act.wait_ge(const_done, 1)

            def norm_apply(i, s, l):
                act.wait_ge(norm_ready[s], norm_ready.at(i, l + 1))
                src = x_in[s] if l == 0 else xs[s]
                for b in range(GROUP):
                    last = act.activation(nat[s][:, b, :], src[:, b, :], ACT.Relu, bias=shift[s][:, b:b + 1],
                                          scale=rstd[s][:, b:b + 1])
                last.then_inc(full[s], 1)

            def copy_turned_lo(i, s, what):
                act.wait_ge(turned_b[s], turned_b.at(i, TURN[what] + 1))
                act.activation(turned[s][:, 1, :, :].rearrange("p c n -> p (c n)"), ps_h[s][:, 1, 0:KC * GROUP * P], ACT.Copy)\
                   .then_inc(copied_b[s], 1)

            def gat_features_hi(i, s, a):
                f = F0 if a == 0 else D
                act.wait_ge(g_made[s], g_made.at(i, a + 1))
                act.activation(g_hi[a][s][:, :, 0:f], ps[s][:, :, 0:f], ACT.Copy, scale=UNSCALE).then_inc(psum_hi[s], 1)

            def gat_exp(i, s, a):
                act.wait_ge(logits[s], logits.at(i, a + 1))
                act.activation(prob[s][:, 0, 0:GROUP * P], za[s][:, :, :].rearrange("p g j -> p (g j)"), ACT.Exp).then_inc(full[s], 1)

            def gat_copy_prob_t_lo(i, s, a):
                act.wait_ge(turned_b[s], turned_b.at(i, TURN[("probs0", "probs3")[a]] + 1))
                act.activation(prob_t[s][:, 0, 1, 0:GROUP * P], ps_h[s][:, 0, 0:GROUP * P], ACT.Copy).then_inc(copied_b[s], 1)

            def agg_copy(i, s):
                for b in range(GROUP):
                    act.wait_ge(agg[s], agg.at(i, b + 1))
                    act.activation(agg_h[s][:, b, :], ps[s][:, b, :], ACT.Copy).then_inc(psum_hi[s], 1)

            def qk_copy(i, s):
                for j in range(4):
                    act.wait_ge(qk[s], qk.at(i, (j // KC + 1) * KC))
                    act.activation(wide[s][:, j, :], qk_out(s, j), ACT.Identity, bias=bqk[:, j:j + 1],
                                   scale=UNSCALE * (float(DH) ** -0.5 if j < KC else 1.0)).then_inc(full[s], 1)

            def v_copy(i, s):
                act.wait_ge(v_made[s], v_made.at(i, GROUP))
                act.activation(v_hi[s][:, :, :, 0:DH], ps[s][:, :, 0:D].rearrange("p g (h d) -> p g h d", h=HEADS), ACT.Copy,
                               scale=UNSCALE).then_inc(psum_hi[s], 1)

            def head_exp(i, s, b):
                for k in range(BANKS):
                    act.wait_ge(row_max[s], row_max.at(i, BANKS * b + k + 1))
                    for j in range(BANK // P):
                        at = slice(j * P, (j + 1) * P)
                        last = act.activation(prob[s][:, k, at], ps[s][:, k, at], ACT.Exp, bias=hmax[s][:, k, j:j + 1])
                    last.then_inc(full[s], 1)

            def head_copy_bank1(i, s, b):
                act.wait_ge(turned_b[s], turned_b.at(i, TURN["heads"] + b + 1))
                act.activation(prob_t[s][:, 1, :, :].rearrange("p k n -> p (k n)"), ps_h[s][:, 1, :], ACT.Copy)\
                   .then_inc(copied_b[s], 1)

            def store(i, s):
                act.wait_ge(x_updated[s], x_updated.at(i, LAYERS))
                act.dma_start(out_groups[i * STREAMS + s], y[s][:, :, :]).then_inc(stored[s], 16)

            run(act, {
                **{f"apply{l}": lambda i, s, l=l: norm_apply(i, s, l) for l in range(LAYERS)},
                "turn0_copy": lambda i, s: copy_turned_lo(i, s, "h0"), "turn2_copy": lambda i, s: copy_turned_lo(i, s, "h2"),
                "turn_out_copy": lambda i, s: copy_turned_lo(i, s, "out"), "turn3_copy": lambda i, s: copy_turned_lo(i, s, "h3"),
                "features0_copy": lambda i, s: gat_features_hi(i, s, 0), "features3_copy": lambda i, s: gat_features_hi(i, s, 1),
                "exp0": lambda i, s: gat_exp(i, s, 0), "exp3": lambda i, s: gat_exp(i, s, 1),
                "turn_probs0_copy": lambda i, s: gat_copy_prob_t_lo(i, s, 0),
                "turn_probs3_copy": lambda i, s: gat_copy_prob_t_lo(i, s, 1),
                "aggregate_copy": agg_copy, "query_key_copy": qk_copy, "values_copy": v_copy,
                "exp_a": lambda i, s: head_exp(i, s, 0), "exp_b": lambda i, s: head_exp(i, s, 1),
                "turn_heads_a_copy": lambda i, s: head_copy_bank1(i, s, 0),
                "turn_heads_b_copy": lambda i, s: head_copy_bank1(i, s, 1),
                "store": store,
            })

        @block.gpsimd
        def _(pool):
            pool.memset(ident[:, :], 0.0).then_inc(ident_ready, 1)
            pool.wait_ge(ident_ready, 1)
            pool.affine_select(out=ident[:, :], in_=ident[:, :], compare_op=ALU.not_equal, fill=1.0, base=0,
                               pattern=[[-1, P]], channel_multiplier=1).then_inc(ident_ready, 1)
            pool.wait_ge(const_done, 1)

            def norm_rsqrt(i, s, l):
                pool.wait_ge(moments[s], moments.at(i, l + 1))
                pool.tensor_tensor(rstd[s][:, :], var[s][:, :], minus_half[:, :], ALU.pow).then_inc(norm_scale[s], 1)
                pool.wait_ge(norm_scale[s], norm_scale.at(i, l + 1))
                pool.tensor_tensor(shift[s][:, :], mean2[s][:, :], rstd[s][:, :], ALU.mult).then_inc(norm_ready[s], 1)

            def split_lo(i, s, what):
                pool.wait_ge(hi_part[s], hi_part.at(i, SPLIT[what] + 1))
                pool.tensor_tensor(nat_lo[s][:, :, :], nat[s][:, :, :], nat_hi[s][:, :, :], ALU.subtract).then_inc(lo_part[s], 1)

            def add_bias(i, s, l, bias):
                pool.wait_ge(full[s], full.at(i, SPLIT[f"h{l}"] + 1))
                pool.tensor_tensor(xs[s][:, :, :], xs[s][:, :, :], bias[:, :].unsqueeze(1).to_broadcast([P, GROUP, D]),
                                   ALU.add).then_inc(bias_added[s], 1)

            def gat_diag_lo(i, s, a):
                pool.wait_ge(steps_done[s], steps_done.at(i, VECTOR_STEPS[3 * a] + 6))
                pool.tensor_tensor(dst_diag[s][:, 1, :, :], ident_h[:, :].unsqueeze(1).to_broadcast([P, GROUP, P]),
                                   dst_h[s][:, 1, :].unsqueeze(2).to_broadcast([P, GROUP, P]), ALU.mult).then_inc(diag_lo[s], 1)

            def gat_prob_lo(i, s, a):
                pool.wait_ge(hi_part[s], hi_part.at(i, SPLIT[("probs0", "probs3")[a]] + 1))
                pool.tensor_tensor(prob_lo[s][:, 0, 0:GROUP * P], prob[s][:, 0, 0:GROUP * P], prob_hi[s][:, 0, 0:GROUP * P], ALU.subtract).then_inc(lo_part[s], 1)

            def qk_split_lo(i, s):
                for j in range(4):
                    pool.wait_ge(hi_part[s], hi_part.at(i, SPLIT["qk"] + j + 1))
                    pool.tensor_tensor(wide_lo[s][:, j, :], wide[s][:, j, :], wide_hi[s][:, j, :], ALU.subtract).then_inc(lo_part[s], 1)

            def head_prob_lo(i, s, b):
                for k in range(BANKS):
                    pool.wait_ge(hi_part[s], hi_part.at(i, SPLIT["heads"] + BANKS * b + k + 1))
                    pool.tensor_tensor(prob_lo[s][:, k, :], prob[s][:, k, :], prob_hi[s][:, k, :], ALU.subtract).then_inc(lo_part[s], 1)

            run(pool, {
                **{f"rsqrt{l}": lambda i, s, l=l: norm_rsqrt(i, s, l) for l in range(LAYERS)},
                "split_lo0": lambda i, s: split_lo(i, s, "h0"), "split_lo1": lambda i, s: split_lo(i, s, "h1"),
                "split_lo2": lambda i, s: split_lo(i, s, "h2"), "split_out_lo": lambda i, s: split_lo(i, s, "out"),
                "split_lo3": lambda i, s: split_lo(i, s, "h3"),
                "bias1": lambda i, s: add_bias(i, s, 1, bias1), "bias2": lambda i, s: add_bias(i, s, 2, bias2),
                "features0_split": lambda i, s: gat_diag_lo(i, s, 0), "features3_split": lambda i, s: gat_diag_lo(i, s, 1),
                "split_probs0": lambda i, s: gat_prob_lo(i, s, 0), "split_probs3": lambda i, s: gat_prob_lo(i, s, 1),
                "query_key_split": qk_split_lo,
                "split_heads_a": lambda i, s: head_prob_lo(i, s, 0), "split_heads_b": lambda i, s: head_prob_lo(i, s, 1),
            })


def kernel(x, adj, L0_gnn_W, L0_gnn_a, L1_gnn_W, L1_gnn_b, L2_gnn_Wq, L2_gnn_bq, L2_gnn_Wk, L2_gnn_bk,
           L2_gnn_Wv, L2_gnn_bv, L2_gnn_Wo, L2_gnn_bo, L3_gnn_W, L3_gnn_a_src, L3_gnn_a_dst):
    import numpy as np
    import concourse.bacc as bacc
    from concourse.bass_utils import run_bass_kernel_spmd

    x, adj, w0, a0, w1, b1, wq, bq, wk, bk, wv, bv, wo, bo, w3, a_src, a_dst = (
        np.asarray(v) for v in (x, adj, L0_gnn_W, L0_gnn_a, L1_gnn_W, L1_gnn_b, L2_gnn_Wq, L2_gnn_bq, L2_gnn_Wk,
                                L2_gnn_bk, L2_gnn_Wv, L2_gnn_bv, L2_gnn_Wo, L2_gnn_bo, L3_gnn_W, L3_gnn_a_src,
                                L3_gnn_a_dst))
    columns = lambda v: v.reshape(-1, P).T
    arrays = {
        "in_x": x, "in_adj": adj, "in_adj_t": adj.T,
        "in_w0": w0, "in_w0_t": w0.T, "in_a0": a0[:, :, 0].T,
        "in_w_i": w1[:, :D].T, "in_w_j": w1[:, D:].T, "in_b1": b1,
        "in_w_q": wq.T, "in_w_k": wk.T, "in_b_qk": np.concatenate([columns(bq), columns(bk)], axis=1),
        "in_w_v": wv.T, "in_b_v": columns(bv), "in_w_o": wo.T, "in_b_o": bo,
        "in_w3": w3, "in_w3_t": w3.T, "in_a3": np.stack([a_src, a_dst], axis=1),
    }
    arrays = {k: np.ascontiguousarray(v) for k, v in arrays.items()}
    nc = bacc.Bacc("TRN2", target_bir_lowering=False, num_devices=1)
    args = [nc.dram_tensor(k, v.shape, mybir.dt.from_np(v.dtype), kind="ExternalInput").ap() for k, v in arrays.items()]
    out = nc.dram_tensor("out", x.shape, F32, kind="ExternalOutput").ap()
    nc.disable_value_cache = True
    build(nc, *args, out)
    return run_bass_kernel_spmd(nc, [arrays], core_ids=[0]).results[0]["out"]
```

```python
from contextlib import ExitStack

import concourse.bass as bass
from concourse import mybir

F32 = mybir.dt.float32
F16 = mybir.dt.float16
BF16 = mybir.dt.bfloat16
ALU = mybir.AluOpType
ACT = mybir.ActivationFunctionType
AX = mybir.AxisListType

P = 128
D = 256
KC = D // P
GROUP = 2
STREAMS = 4
HEADS = 8
DH = D // HEADS
QUADS = P // DH
BANKS = 2
BANK = 512
EPS = 1e-5
SLOPE = 0.2
MASKED = -1e30
WEIGHT_SCALE = 256.0
UNSCALE = 1.0 / WEIGHT_SCALE
F0 = 128
LAYERS = 4

COL_W0, COL_W3 = 0, F0 + 2
COL_WI = COL_W3 + D + 2
COL_WJ, COL_WQ, COL_WK, COL_WV, COL_WO = (COL_WI + D * k for k in range(1, 6))
COLS = COL_WO + D





VECTOR_STEPS = [0, 6, 6, 6 + GROUP, 12 + GROUP]
SPLIT = {"h0": 0, "probs0": 1, "h1": 2, "h2": 3, "qk": 4, "heads": 8, "out": 8 + BANKS * GROUP,
         "h3": 9 + BANKS * GROUP, "probs3": 10 + BANKS * GROUP}
SPLITS = 11 + BANKS * GROUP
PSUM_SPLIT = {"features0": 0, "aggregates": 1, "values": 1 + GROUP, "features3": 2 + GROUP}
FROM_PSUM = 3 + GROUP
TURN = {"h0": 0, "probs0": 1, "h2": 2, "heads": 3, "out": 3 + GROUP, "h3": 4 + GROUP, "probs3": 5 + GROUP}
TURNS = 6 + GROUP



def build(nc, x, adj, adj_t, w0, w0_t, a0, w_i, w_j, b1, w_q, w_k, b_qk, w_v, b_v, w_o, b_o, w3, w3_t, a3, out):
    graphs = x.shape[0]
    steps = graphs // (GROUP * STREAMS)
    assert graphs == steps * GROUP * STREAMS and x.shape[1] == P and x.shape[2] == D
    x_groups = x.rearrange("(g b) n d -> g n b d", b=GROUP)
    out_groups = out.rearrange("(g b) n d -> g n b d", b=GROUP)

    ctx = ExitStack()
    with ctx:
        def sb(name, shape, dt):
            return ctx.enter_context(nc.sbuf_tensor(name, shape, dt))

        def sem(name):
            return ctx.enter_context(nc.semaphore(name))

        def per_stream(name, shape, dt):
            return [sb(f"{name}{s}", shape, dt) for s in range(STREAMS)]

        adj_i = sb("adj_i", [P, 2, P], mybir.dt.int32)
        adj_f = sb("adj_f", [P, 2, P], F32)
        degree = sb("degree", [P, 1], F32)
        mask = sb("mask", [P, 2, P], BF16)
        agg_deg = sb("agg_deg", [P, 2 * P], F16)
        ident = sb("ident", [P, P], F32)
        ident_h = sb("ident_h", [P, P], F16)
        ident_b = sb("ident_b", [P, P], BF16)
        ones_h = sb("ones_h", [P, P], F16)
        minus_half = sb("minus_half", [P, GROUP], F32)
        w_f = sb("w_f", [P, KC, COLS], F32)
        w_hi = sb("w_hi", [P, KC, COLS], F16)
        w_lo = sb("w_lo", [P, KC, COLS], F16)
        w0t_f = sb("w0t_f", [P, D], F32)
        w3t_f = sb("w3t_f", [P, KC, D], F32)
        a0_f = sb("a0_f", [P, 2], F32)
        a3_f = sb("a3_f", [P, KC, 2], F32)
        bqk = sb("bqk", [P, 2 * KC], F32)
        bv_col = sb("bv_col", [P, KC], F32)
        bv_wide = sb("bv_wide", [P, KC, P], F32)
        b1_row = sb("b1_row", [P, D], F32)
        bo_row = sb("bo_row", [P, D], F32)
        bias1 = sb("bias1", [P, D], F32)
        bias2 = sb("bias2", [P, D], F32)

        x_in = per_stream("x_in", [P, GROUP, D], F32)
        xs = per_stream("xs", [P, GROUP, D], F32)
        y = per_stream("y", [P, GROUP, D], F32)
        stats = per_stream("stats", [P, GROUP, 6], F32)
        mean2 = per_stream("mean2", [P, GROUP], F32)
        var = per_stream("var", [P, GROUP], F32)
        m2 = per_stream("m2", [P, GROUP], F32)
        gap = per_stream("gap", [P, GROUP], F32)
        rstd = per_stream("rstd", [P, GROUP], F32)
        shift = per_stream("shift", [P, GROUP], F32)
        nat = per_stream("nat", [P, GROUP, D], F32)
        nat_hi = per_stream("nat_hi", [P, GROUP, D], F16)
        nat_lo = per_stream("nat_lo", [P, GROUP, D], F16)
        turned = per_stream("turned", [P, 2, KC, GROUP * P], F16)
        g_hi = [per_stream("g0_hi", [P, GROUP, F0 + 1], F16), per_stream("g3_hi", [P, GROUP, D + 1], F16)]
        g_lo = [per_stream("g0_lo", [P, GROUP, F0 + 1], F16), per_stream("g3_lo", [P, GROUP, D + 1], F16)]
        src_dst = per_stream("src_dst", [P, GROUP, 2], F32)
        dst_h = per_stream("dst_h", [P, 2, GROUP], F16)
        dst_diag = per_stream("dst_diag", [P, 2, GROUP, P], F16)
        za = per_stream("za", [P, GROUP, P], F32)
        zb = per_stream("zb", [P, GROUP, P], F32)
        gmax = per_stream("gmax", [P, GROUP], F32)
        grec = per_stream("grec", [P, GROUP], F32)
        wide = per_stream("wide", [P, 2 * KC, GROUP * P], F32)
        wide_hi = per_stream("wide_hi", [P, 2 * KC, GROUP * P], F16)
        wide_lo = per_stream("wide_lo", [P, 2 * KC, GROUP * P], F16)
        agg_h, agg_l = ([t[:, :, :].rearrange("p (b k) n -> p b (k n)", b=GROUP) for t in w] for w in (wide_hi, wide_lo))
        prob = per_stream("prob", [P, BANKS, BANK], F32)
        prob_hi = per_stream("prob_hi", [P, BANKS, BANK], F16)
        prob_lo = per_stream("prob_lo", [P, BANKS, BANK], F16)
        prob_t = per_stream("prob_t", [P, BANKS, 2, BANK], F16)
        v_hi = per_stream("v_hi", [P, GROUP, HEADS, DH + 1], F16)
        v_lo = per_stream("v_lo", [P, GROUP, HEADS, DH + 1], F16)
        hmax = per_stream("hmax", [P, BANKS, HEADS // BANKS], F32)
        hrec = per_stream("hrec", [P, HEADS], F32)

        ps = [ctx.enter_context(nc.psum_tensor(f"ps{s}", [P, BANKS, BANK], F32)) for s in range(STREAMS)]
        ps_h = [ps[s][:, :, :].bitcast(F16) for s in range(STREAMS)]

        def qk_out(s, j):
            return ps[s][:, j // KC, (j % KC) * GROUP * P:(j % KC + 1) * GROUP * P]

        loads = sem("constants_loaded")
        ident_ready = sem("ident_ready")
        setup = sem("setup_steps")
        setup_pe = sem("setup_products")
        const_done = sem("constants_ready")

        class Signal:

            def __init__(self, name, per_step):
                self.sem = [sem(f"{name}{s}") for s in range(STREAMS)]
                self.per_step = per_step

            def __getitem__(self, s):
                return self.sem[s]

            def at(self, i, k):
                return i * self.per_step + k

        loaded = Signal("loaded", 16)
        stored = Signal("stored", 16)
        steps_done = Signal("vector_steps", VECTOR_STEPS[LAYERS])
        norm_steps = Signal("norm_steps", 3 * LAYERS)
        moments = Signal("moments", LAYERS)
        norm_scale = Signal("norm_scale", LAYERS)
        norm_ready = Signal("norm_ready", LAYERS)
        full = Signal("full", SPLITS)
        hi_part = Signal("hi_part", SPLITS)
        lo_part = Signal("lo_part", SPLITS)
        psum_hi = Signal("psum_hi", FROM_PSUM)
        psum_lo = Signal("psum_lo", FROM_PSUM)
        turned_a = Signal("turned_a", TURNS)
        turned_b = Signal("turned_b", TURNS)
        copied_a = Signal("copied_a", TURNS)
        copied_b = Signal("copied_b", TURNS)
        x_updated = Signal("x_updated", LAYERS)
        bias_added = Signal("bias_added", 2)
        g_made = Signal("gat_features", 2)
        diag_hi = Signal("diag_hi", 2)
        diag_lo = Signal("diag_lo", 2)
        dst_rows = Signal("dst_rows", 2)
        logits = Signal("logits", 2)
        g_out = Signal("gat_out", 2)
        agg = Signal("aggregated", GROUP)
        update = Signal("update", 2 * GROUP)
        qk = Signal("query_key", 2 * KC)
        v_made = Signal("values", GROUP)
        scores = Signal("scores", GROUP)
        half_scores = Signal("half_scores", GROUP)
        row_max = Signal("row_max", BANKS * GROUP)
        heads_out = Signal("heads_out", GROUP)
        bank_free = Signal("bank_free", GROUP - 1)

        both = range(STREAMS)

        def run(eng, slot):
            def slots(i, first=False, last=False):
                for r in range(STREAMS):
                    def at(part, piece, *which):
                        if not (first and part > r) and not (last and part <= r):
                            piece(i if part <= r else i - 1, (r - part) % STREAMS, *which)
                    slot(at)

            slots(0, first=True)
            with eng.Fori(1, steps) as i:
                slots(i)
            slots(steps, last=True)

        block = ctx.enter_context(nc.Block())

        @block.sync
        def _(sp):
            for dst, src in (
                (adj_i[:, 0, :], adj), (adj_i[:, 1, :], adj_t),
                (w_f[:, :, COL_W0:COL_W0 + F0], w0.rearrange("(c p) n -> p c n", p=P)),
                (w_f[:, :, COL_W3:COL_W3 + D], w3.rearrange("(c p) n -> p c n", p=P)),
                (w_f[:, :, COL_WI:COL_WI + D], w_i.rearrange("(c p) n -> p c n", p=P)),
                (w_f[:, :, COL_WJ:COL_WJ + D], w_j.rearrange("(c p) n -> p c n", p=P)),
                (w_f[:, :, COL_WQ:COL_WQ + D], w_q.rearrange("(c p) n -> p c n", p=P)),
                (w_f[:, :, COL_WK:COL_WK + D], w_k.rearrange("(c p) n -> p c n", p=P)),
                (w_f[:, :, COL_WV:COL_WV + D], w_v.rearrange("(c p) n -> p c n", p=P)),
                (w_f[:, :, COL_WO:COL_WO + D], w_o.rearrange("(c p) n -> p c n", p=P)),
                (w0t_f[:, :], w0_t), (w3t_f[:, :, :], w3_t.rearrange("(c p) n -> p c n", p=P)),
                (a0_f[:, :], a0), (a3_f[:, :, :], a3.rearrange("(c p) k -> p c k", p=P)),
                (bqk[:, :], b_qk), (bv_col[:, :], b_v),
                (b1_row[:, :], b1.partition_broadcast(P)), (bo_row[:, :], b_o.partition_broadcast(P)),
            ):
                sp.dma_start(dst, src).then_inc(loads, 16)
            for s in both:
                sp.dma_start(x_in[s][:, :, :], x_groups[s]).then_inc(loaded[s], 16)
            with sp.Fori(1, steps) as i:
                for s in both:
                    sp.wait_ge(x_updated[s], x_updated.at(i - 1, 1))
                    sp.dma_start(x_in[s][:, :, :], x_groups[i * STREAMS + s]).then_inc(loaded[s], 16)
            for s in both:
                sp.wait_ge(stored[s], 16 + stored.at(steps - 1, 16))

        n_loads = 18 * 16

        @block.tensor
        def _(pe):
            pe.wait_ge(loads, n_loads)
            pe.wait_ge(setup, 2)
            for c in range(KC):
                pe.matmul(ps[0][:, 0, 2 * c:2 * c + 2], w0t_f[:, c * P:(c + 1) * P], a0_f[:, :], start=True, stop=True)
            for c in range(KC):
                for e in range(KC):
                    pe.matmul(ps[0][:, 1, 2 * c:2 * c + 2], w3t_f[:, e, c * P:(c + 1) * P], a3_f[:, e, :],
                              start=(e == 0), stop=(e == KC - 1))
            for c in range(KC):
                last = pe.matmul(ps[1][:, 0, 0:D], bv_wide[:, c, :], w_f[:, c, COL_WO:COL_WO + D],
                                 start=(c == 0), stop=(c == KC - 1))
            last.then_inc(setup_pe, 1)
            pe.wait_ge(const_done, 1)

            def product(out_ap, left, right, start=True, stop=True):
                for c in range(KC):
                    (lh, ll), (rh, rl) = left(c), right(c)
                    pe.matmul(out_ap, lh, rh, start=start and c == 0, stop=False)
                    pe.matmul(out_ap, lh, rl, start=False, stop=False)
                    last = pe.matmul(out_ap, ll, rh, start=False, stop=stop and c == KC - 1)
                return last

            def weights(col, n):
                return lambda c: (w_hi[:, c, col:col + n], w_lo[:, c, col:col + n])

            def turned_cols(s, b, n):
                return lambda c: (turned[s][:, 0, c, b * P:b * P + n], turned[s][:, 1, c, b * P:b * P + n])

            def turn_hi(i, s, what):
                if what == "h0" and not (isinstance(i, int) and i == 0):
                    pe.wait_ge(x_updated[s], x_updated.at(i, 0))
                pe.wait_ge(hi_part[s], hi_part.at(i, SPLIT[what] + 1))
                for c in range(KC):
                    for b in range(GROUP):
                        last = pe.transpose(ps_h[s][:, 0, (c * GROUP + b) * P:(c * GROUP + b + 1) * P],
                                            nat_hi[s][:, b, c * P:(c + 1) * P], ident_h[:, :])
                last.then_inc(turned_a[s], 1)

            def turn_lo(i, s, what):
                pe.wait_ge(lo_part[s], lo_part.at(i, SPLIT[what] + 1))
                for c in range(KC):
                    for b in range(GROUP):
                        last = pe.transpose(ps_h[s][:, 1, (c * GROUP + b) * P:(c * GROUP + b + 1) * P],
                                            nat_lo[s][:, b, c * P:(c + 1) * P], ident_h[:, :])
                last.then_inc(turned_b[s], 1)

            def wait_turned(i, s, what):
                pe.wait_ge(copied_a[s], copied_a.at(i, TURN[what] + 1))
                pe.wait_ge(copied_b[s], copied_b.at(i, TURN[what] + 1))

            def features(i, s, a):
                f, col = (F0, COL_W0) if a == 0 else (D, COL_W3)
                wait_turned(i, s, ("h0", "h3")[a])
                for b in range(GROUP):
                    last = product(ps[s][:, b, 0:f + 2], turned_cols(s, b, P), weights(col, f + 2))
                last.then_inc(g_made[s], 1)

            def dst_rows_sum(i, s, a):
                pe.wait_ge(psum_lo[s], psum_lo.at(i, PSUM_SPLIT[("features0", "features3")[a]] + 1))
                pe.wait_ge(diag_hi[s], diag_hi.at(i, a + 1))
                pe.matmul(ps[s][:, 0, 0:GROUP * P], ident_b[:, :], mask[:, :, :].rearrange("p g j -> p (g j)"), start=True, stop=False)
                pe.matmul(ps[s][:, 0, 0:GROUP * P], ones_h[:, :], dst_diag[s][:, 0, :, :].rearrange("p g j -> p (g j)"),
                          start=False, stop=False)
                pe.wait_ge(diag_lo[s], diag_lo.at(i, a + 1))
                pe.matmul(ps[s][:, 0, 0:GROUP * P], ones_h[:, :], dst_diag[s][:, 1, :, :].rearrange("p g j -> p (g j)"),
                          start=False, stop=True).then_inc(dst_rows[s], 1)

            def turn_probs(i, s, a, half):
                part, src, done, bank = ((hi_part, prob_hi, turned_a, 1), (lo_part, prob_lo, turned_b, 0))[half]
                pe.wait_ge(part[s], part.at(i, SPLIT[("probs0", "probs3")[a]] + 1))
                for b in range(GROUP):
                    last = pe.transpose(ps_h[s][:, bank, b * P:(b + 1) * P], src[s][:, 0, b * P:(b + 1) * P], ident_h[:, :])
                last.then_inc(done[s], 1)

            def gat_sum(i, s, a):
                f = F0 if a == 0 else D
                wait_turned(i, s, ("probs0", "probs3")[a])
                for b in range(GROUP):
                    ph, pl = (prob_t[s][:, 0, k, b * P:(b + 1) * P] for k in range(2))
                    o = ps[s][:, b, 0:f + 1]
                    pe.matmul(o, ph, g_hi[a][s][:, b, :], start=True, stop=False)
                    pe.matmul(o, ph, g_lo[a][s][:, b, :], start=False, stop=False)
                    last = pe.matmul(o, pl, g_hi[a][s][:, b, :], start=False, stop=True)
                last.then_inc(g_out[s], 1)

            def aggregate(i, s, b):
                pe.wait_ge(hi_part[s], hi_part.at(i, SPLIT["h1"] + 1))
                pe.wait_ge(lo_part[s], lo_part.at(i, SPLIT["h1"] + 1))
                for c in range(KC):
                    o = ps[s][:, b, c * 2 * P:(c + 1) * 2 * P]
                    pe.matmul(o, nat_hi[s][:, b, c * P:(c + 1) * P], agg_deg[:, :], start=True, stop=False)
                    last = pe.matmul(o, nat_lo[s][:, b, c * P:(c + 1) * P], agg_deg[:, :], start=False, stop=True)
                last.then_inc(agg[s], 1)

            def messages(i, s, b):
                pe.wait_ge(psum_hi[s], psum_hi.at(i, PSUM_SPLIT["aggregates"] + b + 1))
                pe.wait_ge(psum_lo[s], psum_lo.at(i, PSUM_SPLIT["aggregates"] + b + 1))
                for part, col in ((0, COL_WJ), (1, COL_WI)):
                    def left(c):
                        at = slice(c * 2 * P + part * P, c * 2 * P + (part + 1) * P)
                        return agg_h[s][:, b, at], agg_l[s][:, b, at]
                    last = product(ps[s][:, b, 0:D], left, weights(col, D), start=(part == 0), stop=(part == 1))
                last.then_inc(update[s], 1)

            def query_key(i, s, j):
                wait_turned(i, s, "h2")
                col = (COL_WQ, COL_WK)[j // KC] + (j % KC) * P
                product(qk_out(s, j), weights(col, P), turned_cols(s, 0, GROUP * P)).then_inc(qk[s], 1)

            def values(i, s, b):
                pe.wait_ge(full[s], full.at(i, SPLIT["qk"] + KC * (b + 1)))
                product(ps[s][:, b, 0:D], turned_cols(s, b, P), weights(COL_WV, D)).then_inc(v_made[s], 1)

            def head_scores(i, s, b, half):
                if half == 0 and b == 0:
                    pe.wait_ge(hi_part[s], hi_part.at(i, SPLIT["qk"] + 2 * KC))
                    pe.wait_ge(lo_part[s], lo_part.at(i, SPLIT["qk"] + 2 * KC))
                    pe.wait_ge(psum_hi[s], psum_hi.at(i, PSUM_SPLIT["values"] + 1))
                    pe.wait_ge(psum_lo[s], psum_lo.at(i, PSUM_SPLIT["values"] + 1))
                elif half == 0:
                    pe.wait_ge(bank_free[s], bank_free.at(i, b))
                for k in range(BANKS):
                    pe.matmul(ps[s][:, k, half * KC * P:(half + 1) * KC * P], ident_b[:, :],
                              mask[:, :, :].rearrange("p g j -> p (g j)"), start=True, stop=False)
                if half == 1:
                    pe.wait_ge(half_scores[s], half_scores.at(i, b + 1))
                for c in range(KC):
                    for t, (q, kk) in enumerate(((wide_hi, wide_hi), (wide_hi, wide_lo), (wide_lo, wide_hi))):
                        for k in range(BANKS):
                            a = half * BANKS + k
                            rows = slice(a * DH, (a + 1) * DH)
                            last = pe.matmul(ps[s][:, k, (half * KC + c) * P:(half * KC + c + 1) * P],
                                             q[s][rows, c, b * P:(b + 1) * P], kk[s][rows, KC + c, b * P:(b + 1) * P],
                                             start=False, stop=(t == 2 and c == KC - 1))
                last.then_inc((half_scores, scores)[half][s], 1)

            def turn_heads(i, s, b, k):
                pe.wait_ge(hi_part[s], hi_part.at(i, SPLIT["heads"] + BANKS * b + k + 1))
                pe.wait_ge(lo_part[s], lo_part.at(i, SPLIT["heads"] + BANKS * b + k + 1))
                for part, src in enumerate((prob_hi, prob_lo)):
                    for j in range(BANK // P):
                        last = pe.transpose(ps_h[s][:, k, part * BANK + j * P:part * BANK + (j + 1) * P],
                                            src[s][:, k, j * P:(j + 1) * P], ident_h[:, :])
                last.then_inc((turned_a, turned_b)[k][s], 1)

            def sum_heads(i, s, b):
                pe.wait_ge(copied_a[s], copied_a.at(i, TURN["heads"] + b + 1))
                pe.wait_ge(copied_b[s], copied_b.at(i, TURN["heads"] + b + 1))
                for h in range(HEADS):
                    c, a = h // QUADS, h % QUADS
                    o = ps[s][:, 0, h * (DH + 1):(h + 1) * (DH + 1)]
                    col = ((a // BANKS) * KC + c) * P
                    ph, pl = (prob_t[s][:, a % BANKS, part, col:col + P] for part in range(2))
                    pe.matmul(o, ph, v_hi[s][:, b, h, :], start=True, stop=False)
                    pe.matmul(o, ph, v_lo[s][:, b, h, :], start=False, stop=False)
                    last = pe.matmul(o, pl, v_hi[s][:, b, h, :], start=False, stop=True)
                last.then_inc(heads_out[s], 1)

            def project(i, s, b):
                wait_turned(i, s, "out")
                product(ps[s][:, b, 0:D], turned_cols(s, b, P), weights(COL_WO, D)).then_inc(update[s], 1)

            def slot(at):
                at(3, turn_heads, 1, 1)
                at(2, values, 0)
                at(4, turn_lo, "h3")
                at(2, values, 1)
                at(3, sum_heads, 1)
                at(4, features, 1)
                at(2, head_scores, 0, 0)
                at(2, head_scores, 0, 1)
                at(1, aggregate, 0)
                at(1, aggregate, 1)
                at(4, dst_rows_sum, 1)
                at(3, turn_hi, "out")
                at(1, messages, 0)
                at(1, messages, 1)
                at(3, turn_lo, "out")
                at(4, turn_probs, 1, 0)
                at(2, turn_heads, 0, 0)
                at(2, turn_heads, 0, 1)
                at(3, project, 0)
                at(4, turn_probs, 1, 1)
                at(3, project, 1)
                at(2, sum_heads, 0)
                at(4, gat_sum, 1)
                at(2, head_scores, 1, 0)
                at(1, turn_hi, "h2")
                at(2, head_scores, 1, 1)
                at(1, turn_lo, "h2")
                at(0, turn_hi, "h0")
                at(0, turn_lo, "h0")
                at(0, features, 0)
                at(1, query_key, 0)
                at(1, query_key, 1)
                at(0, dst_rows_sum, 0)
                at(1, query_key, 2)
                at(1, query_key, 3)
                at(2, turn_heads, 1, 0)
                at(3, turn_hi, "h3")
                at(0, turn_probs, 0, 0)
                at(0, turn_probs, 0, 1)
                at(0, gat_sum, 0)
            run(pe, slot)

        @block.vector
        def _(dve):
            dve.wait_ge(loads, n_loads)
            n = 0

            def link(ins):
                nonlocal n
                ins.then_inc(setup, 1)
                n += 1
                dve.wait_ge(setup, n)

            for s in both:
                dve.memset(y[s][:, :, :], 0.0).then_inc(stored[s], 16)
            link(dve.memset(bv_wide[:, :, :], 0.0))
            for c in range(KC):
                last = dve.tensor_scalar(bv_wide[:, c, :], bv_wide[:, c, :], bv_col[:, c:c + 1], None, ALU.add)
            link(last)
            link(dve.tensor_copy(adj_f[:, :, :], adj_i[:, :, :]))
            dve.tensor_copy(agg_deg[:, 0:P], adj_f[:, 1, :])
            for g in range(2):
                dve.tensor_scalar(mask[:, g, :], adj_f[:, 0, :], -1.0, -MASKED, ALU.add, ALU.mult)
            link(dve.tensor_reduce(degree[:, :], adj_f[:, 0, :], AX.X, ALU.add))
            dve.tensor_scalar(bias1[:, :], b1_row[:, :], degree[:, 0:1], None, ALU.mult)
            dve.memset(minus_half[:, :], -0.5)
            dve.memset(ones_h[:, :], 1.0)
            for s in both:
                dve.memset(g_hi[0][s][:, :, F0:F0 + 1], 1.0)
                dve.memset(g_hi[1][s][:, :, D:D + 1], 1.0)
                dve.memset(g_lo[0][s][:, :, F0:F0 + 1], 0.0)
                dve.memset(g_lo[1][s][:, :, D:D + 1], 0.0)
                dve.memset(v_hi[s][:, :, :, DH:DH + 1], 1.0)
                dve.memset(v_lo[s][:, :, :, DH:DH + 1], 0.0)
            dve.tensor_scalar(bqk[:, 0:KC], bqk[:, 0:KC], float(DH) ** -0.5, None, ALU.mult)
            dve.wait_ge(setup_pe, 1)
            dve.tensor_copy(w_f[:, :, COL_W0 + F0:COL_W0 + F0 + 2], ps[0][:, 0, 0:2 * KC].rearrange("p (c k) -> p c k", c=KC))
            dve.tensor_copy(w_f[:, :, COL_W3 + D:COL_W3 + D + 2], ps[0][:, 1, 0:2 * KC].rearrange("p (c k) -> p c k", c=KC))
            link(dve.tensor_tensor(bias2[:, :], ps[1][:, 0, 0:D], bo_row[:, :], ALU.add))
            link(dve.tensor_scalar(w_f[:, :, :], w_f[:, :, :], WEIGHT_SCALE, None, ALU.mult))
            link(dve.tensor_copy(w_hi[:, :, :], w_f[:, :, :]))
            dve.tensor_tensor(w_lo[:, :, :], w_f[:, :, :], w_hi[:, :, :], ALU.subtract)
            dve.wait_ge(ident_ready, 2)
            dve.tensor_copy(ident_h[:, :], ident[:, :])
            dve.tensor_copy(ident_b[:, :], ident[:, :])
            dve.tensor_scalar(agg_deg[:, P:2 * P], ident[:, :], degree[:, 0:1], None, ALU.mult).then_inc(const_done, 1)
            dve.wait_ge(const_done, 1)

            def src(l, s):
                return (x_in if l == 0 else xs)[s]

            def norm_stats(i, s, l):
                if l == 0:
                    dve.wait_ge(loaded[s], loaded.at(i, 16))
                else:
                    dve.wait_ge(x_updated[s], x_updated.at(i, l))
                for b in range(GROUP):
                    last = dve.bn_stats(stats[s][:, b, :], (x_in if l == 0 else xs)[s][:, b, :])
                last.then_inc(norm_steps[s], 1)

            def moments_a(i, s, l):
                even, odd = stats[s][:, :, 0:3], stats[s][:, :, 3:6]
                dve.wait_ge(norm_steps[s], norm_steps.at(i, 3 * l + 1))
                dve.tensor_tensor(gap[s][:, :], even[:, :, 1], odd[:, :, 1], ALU.subtract)
                dve.tensor_tensor(mean2[s][:, :], even[:, :, 1], odd[:, :, 1], ALU.add)
                dve.tensor_tensor(m2[s][:, :], even[:, :, 2], odd[:, :, 2], ALU.add).then_inc(norm_steps[s], 1)

            def moments_b(i, s, l):
                dve.wait_ge(norm_steps[s], norm_steps.at(i, 3 * l + 2))
                dve.scalar_tensor_tensor(gap[s][:, :], gap[s][:, :], 0.25, gap[s][:, :], ALU.mult, ALU.mult)
                dve.tensor_scalar(m2[s][:, :], m2[s][:, :], 1.0 / D, EPS, ALU.mult, ALU.add)
                dve.tensor_scalar(mean2[s][:, :], mean2[s][:, :], -0.5, None, ALU.mult).then_inc(norm_steps[s], 1)

            def moments_c(i, s, l):
                dve.wait_ge(norm_steps[s], norm_steps.at(i, 3 * l + 3))
                dve.tensor_tensor(var[s][:, :], m2[s][:, :], gap[s][:, :], ALU.add).then_inc(moments[s], 1)

            def split_hi(i, s, what):
                dve.wait_ge(full[s], full.at(i, SPLIT[what] + 1))
                dve.tensor_copy(nat_hi[s][:, :, :], nat[s][:, :, :]).then_inc(hi_part[s], 1)

            def copy_turned_hi(i, s, what):
                dve.wait_ge(turned_a[s], turned_a.at(i, TURN[what] + 1))
                dve.tensor_copy(turned[s][:, 0, :, :].rearrange("p c n -> p (c n)"), ps_h[s][:, 0, 0:KC * GROUP * P])\
                   .then_inc(copied_a[s], 1)

            def dst_cols(i, s, a):
                f = F0 if a == 0 else D
                dve.wait_ge(g_made[s], g_made.at(i, a + 1))
                dve.tensor_scalar(src_dst[s][:, :, :], ps[s][:, :, f:f + 2], UNSCALE, None, ALU.mult).then_inc(steps_done[s], 1)

            def dst_hi(i, s, a):
                dve.wait_ge(steps_done[s], steps_done.at(i, VECTOR_STEPS[3 * a] + 1))
                dve.tensor_copy(dst_h[s][:, 0, :], src_dst[s][:, :, 1]).then_inc(steps_done[s], 1)

            def dst_lo(i, s, a):
                dve.wait_ge(steps_done[s], steps_done.at(i, VECTOR_STEPS[3 * a] + 2))
                dve.tensor_tensor(dst_h[s][:, 1, :], src_dst[s][:, :, 1], dst_h[s][:, 0, :], ALU.subtract).then_inc(steps_done[s], 1)
                dve.tensor_tensor(dst_diag[s][:, 0, :, :], ident_h[:, :].unsqueeze(1).to_broadcast([P, GROUP, P]),
                                  dst_h[s][:, 0, :].unsqueeze(2).to_broadcast([P, GROUP, P]), ALU.mult).then_inc(diag_hi[s], 1)

            def features_lo(i, s, a):
                f = F0 if a == 0 else D
                dve.wait_ge(psum_hi[s], psum_hi.at(i, PSUM_SPLIT[("features0", "features3")[a]] + 1))
                last = dve.scalar_tensor_tensor(g_lo[a][s][:, :, 0:f], ps[s][:, :, 0:f], UNSCALE, g_hi[a][s][:, :, 0:f],
                                                ALU.mult, ALU.subtract)
                if a == 0:
                    last = dve.scalar_tensor_tensor(xs[s][:, :, F0:D], ps[s][:, :, 0:F0], UNSCALE, x_in[s][:, :, F0:D],
                                                    ALU.mult, ALU.add)
                last.then_inc(psum_lo[s], 1)

            def logits_sum(i, s, a):
                dve.wait_ge(dst_rows[s], dst_rows.at(i, a + 1))
                dve.tensor_tensor(za[s][:, :, :], ps[s][:, 0, 0:GROUP * P].rearrange("p (g j) -> p g j", g=GROUP),
                                  src_dst[s][:, :, 0:1].to_broadcast([P, GROUP, P]), ALU.add).then_inc(steps_done[s], 1)

            def logits_leaky(i, s, a):
                dve.wait_ge(steps_done[s], steps_done.at(i, VECTOR_STEPS[3 * a] + 4))
                dve.scalar_tensor_tensor(zb[s][:, :, :], za[s][:, :, :], SLOPE, za[s][:, :, :], ALU.mult, ALU.max)\
                   .then_inc(steps_done[s], 1)

            def logits_max(i, s, a):
                dve.wait_ge(steps_done[s], steps_done.at(i, VECTOR_STEPS[3 * a] + 5))
                dve.tensor_reduce(gmax[s][:, :], zb[s][:, :, :], AX.X, ALU.max, negate=True).then_inc(logits[s], 1)

            def copy_probs(i, s, a):
                dve.wait_ge(turned_a[s], turned_a.at(i, TURN[("probs0", "probs3")[a]] + 1))
                dve.tensor_copy(prob_t[s][:, 0, 0, 0:GROUP * P], ps_h[s][:, 1, 0:GROUP * P]).then_inc(copied_a[s], 1)

            def invert_sums(i, s, a):
                dve.wait_ge(g_out[s], g_out.at(i, a + 1))
                dve.reciprocal(grec[s][:, :], ps[s][:, :, F0 if a == 0 else D]).then_inc(steps_done[s], 1)

            def gat_residual(i, s, a):
                f = F0 if a == 0 else D
                dve.wait_ge(steps_done[s], steps_done.at(i, VECTOR_STEPS[3 * a] + 6))
                if a == 1:
                    dve.wait_ge(stored[s], 16 + stored.at(i, 0))
                old, new = ((x_in, xs) if a == 0 else (xs, y))
                for b in range(GROUP):
                    last = dve.scalar_tensor_tensor(new[s][:, b, 0:f], ps[s][:, b, 0:f], grec[s][:, b:b + 1], old[s][:, b, 0:f],
                                                    ALU.mult, ALU.add)
                last.then_inc(x_updated[s], 1)

            def aggregates_lo(i, s, b):
                dve.wait_ge(psum_hi[s], psum_hi.at(i, PSUM_SPLIT["aggregates"] + b + 1))
                dve.tensor_tensor(agg_l[s][:, b, :], ps[s][:, b, :], agg_h[s][:, b, :], ALU.subtract).then_inc(psum_lo[s], 1)

            def linear_residual(i, s, l):
                dve.wait_ge(bias_added[s], bias_added.at(i, l))
                dve.wait_ge(update[s], update.at(i, l * GROUP))
                dve.scalar_tensor_tensor(xs[s][:, :, :], ps[s][:, :, 0:D], UNSCALE, xs[s][:, :, :], ALU.mult, ALU.add)\
                   .then_inc(x_updated[s], 1)

            def values_lo(i, s):
                dve.wait_ge(psum_hi[s], psum_hi.at(i, PSUM_SPLIT["values"] + 1))
                for b in range(GROUP):
                    last = dve.scalar_tensor_tensor(v_lo[s][:, b, :, 0:DH], ps[s][:, b, 0:D].rearrange("p (h d) -> p h d", h=HEADS),
                                                    UNSCALE, v_hi[s][:, b, :, 0:DH], ALU.mult, ALU.subtract)
                last.then_inc(psum_lo[s], 1)

            def heads_max(i, s, b, k):
                dve.wait_ge(scores[s], scores.at(i, b + 1))
                dve.tensor_reduce(hmax[s][:, k, :], ps[s][:, k, :].rearrange("p (j k) -> p j k", k=P), AX.X, ALU.max,
                                  negate=True).then_inc(row_max[s], 1)

            def heads_hi(i, s, b, k):
                dve.wait_ge(full[s], full.at(i, SPLIT["heads"] + BANKS * b + k + 1))
                dve.tensor_copy(prob_hi[s][:, k, :], prob[s][:, k, :]).then_inc(hi_part[s], 1)

            def copy_heads(i, s, b):
                dve.wait_ge(turned_a[s], turned_a.at(i, TURN["heads"] + b + 1))
                dve.tensor_copy(prob_t[s][:, 0, :, :].rearrange("p k n -> p (k n)"), ps_h[s][:, 0, :]).then_inc(copied_a[s], 1)

            def head_cols(s):
                return ps[s][:, 0, 0:HEADS * (DH + 1)].rearrange("p (h d) -> p h d", h=HEADS)

            def invert_heads(i, s, b):
                dve.wait_ge(heads_out[s], heads_out.at(i, b + 1))
                dve.reciprocal(hrec[s][:, :], head_cols(s)[:, :, DH]).then_inc(steps_done[s], 1)

            def normalise(i, s, b):
                dve.wait_ge(steps_done[s], steps_done.at(i, VECTOR_STEPS[2] + b + 1))
                dve.tensor_tensor(nat[s][:, b, :].rearrange("p (h d) -> p h d", h=HEADS), head_cols(s)[:, :, 0:DH],
                                  hrec[s][:, :].unsqueeze(2).to_broadcast([P, HEADS, DH]), ALU.mult)\
                   .then_inc((full if b == GROUP - 1 else bank_free)[s], 1)

            def slot(at):
                at(1, copy_probs, 0)
                at(0, norm_stats, 0)
                at(4, copy_turned_hi, "h3")
                at(1, invert_sums, 0)
                at(1, gat_residual, 0)
                at(1, norm_stats, 1)
                at(1, moments_a, 1)
                at(1, moments_b, 1)
                at(1, moments_c, 1)
                at(0, moments_a, 0)
                at(0, moments_b, 0)
                at(3, invert_heads, 1)
                at(2, values_lo)
                at(3, normalise, 1)
                at(4, dst_cols, 1)
                at(4, dst_hi, 1)
                at(1, split_hi, "h1")
                at(3, split_hi, "out")
                at(4, dst_lo, 1)
                at(4, features_lo, 1)
                at(2, heads_max, 0, 0)
                at(0, moments_c, 0)
                at(2, heads_max, 0, 1)
                at(1, aggregates_lo, 0)
                at(4, logits_sum, 1)
                at(1, aggregates_lo, 1)
                at(2, heads_hi, 0, 0)
                at(4, logits_leaky, 1)
                at(4, logits_max, 1)
                at(2, heads_hi, 0, 1)
                at(3, copy_turned_hi, "out")
                at(1, linear_residual, 1)
                at(1, norm_stats, 2)
                at(1, moments_a, 2)
                at(1, moments_b, 2)
                at(1, moments_c, 2)
                at(2, copy_heads, 0)
                at(4, copy_probs, 1)
                at(3, linear_residual, 2)
                at(2, invert_heads, 0)
                at(2, normalise, 0)
                at(1, split_hi, "h2")
                at(3, norm_stats, 3)
                at(0, split_hi, "h0")
                at(4, invert_sums, 1)
                at(3, moments_a, 3)
                at(4, gat_residual, 1)
                at(2, heads_max, 1, 0)
                at(0, copy_turned_hi, "h0")
                at(1, copy_turned_hi, "h2")
                at(3, moments_b, 3)
                at(3, moments_c, 3)
                at(2, heads_max, 1, 1)
                at(0, dst_cols, 0)
                at(0, dst_hi, 0)
                at(0, dst_lo, 0)
                at(0, features_lo, 0)
                at(2, heads_hi, 1, 0)
                at(3, split_hi, "h3")
                at(0, logits_sum, 0)
                at(0, logits_leaky, 0)
                at(0, logits_max, 0)
                at(2, heads_hi, 1, 1)
                at(2, copy_heads, 1)
            run(dve, slot)

        @block.scalar
        def _(act):
            act.wait_ge(const_done, 1)

            def norm_apply(i, s, l):
                act.wait_ge(norm_ready[s], norm_ready.at(i, l + 1))
                src = x_in[s] if l == 0 else xs[s]
                for b in range(GROUP):
                    last = act.activation(nat[s][:, b, :], src[:, b, :], ACT.Relu, bias=shift[s][:, b:b + 1],
                                          scale=rstd[s][:, b:b + 1])
                last.then_inc(full[s], 1)

            def copy_turned_lo(i, s, what):
                act.wait_ge(turned_b[s], turned_b.at(i, TURN[what] + 1))
                act.activation(turned[s][:, 1, :, :].rearrange("p c n -> p (c n)"), ps_h[s][:, 1, 0:KC * GROUP * P], ACT.Copy)\
                   .then_inc(copied_b[s], 1)

            def features_hi(i, s, a):
                f = F0 if a == 0 else D
                act.wait_ge(steps_done[s], steps_done.at(i, VECTOR_STEPS[3 * a] + 1))
                act.activation(g_hi[a][s][:, :, 0:f], ps[s][:, :, 0:f], ACT.Copy, scale=UNSCALE).then_inc(psum_hi[s], 1)

            def gat_exp(i, s, a):
                act.wait_ge(logits[s], logits.at(i, a + 1))
                for dst, done in ((prob_hi, hi_part), (prob, full)):
                    for b in range(GROUP):
                        last = act.activation(dst[s][:, 0, b * P:(b + 1) * P], zb[s][:, b, :], ACT.Exp, bias=gmax[s][:, b:b + 1])
                    last.then_inc(done[s], 1)

            def copy_probs_lo(i, s, a):
                act.wait_ge(turned_b[s], turned_b.at(i, TURN[("probs0", "probs3")[a]] + 1))
                act.activation(prob_t[s][:, 0, 1, 0:GROUP * P], ps_h[s][:, 0, 0:GROUP * P], ACT.Copy).then_inc(copied_b[s], 1)

            def aggregates_hi(i, s, b):
                act.wait_ge(agg[s], agg.at(i, b + 1))
                act.activation(agg_h[s][:, b, :], ps[s][:, b, :], ACT.Copy).then_inc(psum_hi[s], 1)

            def query_key_copy(i, s, j):
                act.wait_ge(qk[s], qk.at(i, (j // KC + 1) * KC))
                for dst, done in ((wide_hi, hi_part), (wide, full)):
                    act.activation(dst[s][:, j, :], qk_out(s, j), ACT.Identity, bias=bqk[:, j:j + 1],
                                   scale=UNSCALE * (float(DH) ** -0.5 if j < KC else 1.0)).then_inc(done[s], 1)

            def values_hi(i, s):
                act.wait_ge(v_made[s], v_made.at(i, GROUP))
                act.activation(v_hi[s][:, :, :, 0:DH], ps[s][:, :, 0:D].rearrange("p g (h d) -> p g h d", h=HEADS), ACT.Copy,
                               scale=UNSCALE).then_inc(psum_hi[s], 1)

            def heads_exp(i, s, b, k):
                act.wait_ge(row_max[s], row_max.at(i, BANKS * b + k + 1))
                for j in range(BANK // P):
                    at = slice(j * P, (j + 1) * P)
                    last = act.activation(prob[s][:, k, at], ps[s][:, k, at], ACT.Exp, bias=hmax[s][:, k, j:j + 1])
                last.then_inc(full[s], 1)

            def copy_heads_1(i, s, b):
                act.wait_ge(turned_b[s], turned_b.at(i, TURN["heads"] + b + 1))
                act.activation(prob_t[s][:, 1, :, :].rearrange("p k n -> p (k n)"), ps_h[s][:, 1, :], ACT.Copy)\
                   .then_inc(copied_b[s], 1)

            def store(i, s):
                act.wait_ge(x_updated[s], x_updated.at(i, LAYERS))
                act.dma_start(out_groups[i * STREAMS + s], y[s][:, :, :]).then_inc(stored[s], 16)

            def slot(at):
                at(2, query_key_copy, 2)
                at(2, query_key_copy, 3)
                at(3, copy_heads_1, 1)
                at(4, copy_turned_lo, "h3")
                at(2, values_hi)
                at(1, norm_apply, 1)
                at(4, features_hi, 1)
                at(1, aggregates_hi, 0)
                at(1, aggregates_hi, 1)
                at(2, heads_exp, 0, 0)
                at(2, heads_exp, 0, 1)
                at(4, gat_exp, 1)
                at(3, copy_turned_lo, "out")
                at(2, copy_heads_1, 0)
                at(4, copy_probs_lo, 1)
                at(1, norm_apply, 2)
                at(0, norm_apply, 0)
                at(1, copy_turned_lo, "h2")
                at(0, copy_turned_lo, "h0")
                at(2, heads_exp, 1, 0)
                at(0, features_hi, 0)
                at(3, norm_apply, 3)
                at(1, query_key_copy, 0)
                at(2, heads_exp, 1, 1)
                at(4, store)
                at(0, gat_exp, 0)
                at(1, query_key_copy, 1)
                at(0, copy_probs_lo, 0)
            run(act, slot)

        @block.gpsimd
        def _(pool):
            pool.memset(ident[:, :], 0.0).then_inc(ident_ready, 1)
            pool.wait_ge(ident_ready, 1)
            pool.affine_select(out=ident[:, :], in_=ident[:, :], compare_op=ALU.not_equal, fill=1.0, base=0,
                               pattern=[[-1, P]], channel_multiplier=1).then_inc(ident_ready, 1)
            pool.wait_ge(const_done, 1)

            def norm_pow(i, s, l):
                pool.wait_ge(moments[s], moments.at(i, l + 1))
                pool.tensor_tensor(rstd[s][:, :], var[s][:, :], minus_half[:, :], ALU.pow).then_inc(norm_scale[s], 1)

            def norm_shift(i, s, l):
                pool.wait_ge(norm_scale[s], norm_scale.at(i, l + 1))
                pool.tensor_tensor(shift[s][:, :], mean2[s][:, :], rstd[s][:, :], ALU.mult).then_inc(norm_ready[s], 1)

            def split_lo(i, s, what):
                pool.wait_ge(hi_part[s], hi_part.at(i, SPLIT[what] + 1))
                pool.tensor_tensor(nat_lo[s][:, :, :], nat[s][:, :, :], nat_hi[s][:, :, :], ALU.subtract).then_inc(lo_part[s], 1)

            def add_bias(i, s, l, bias):
                pool.wait_ge(full[s], full.at(i, SPLIT[f"h{l}"] + 1))
                pool.tensor_tensor(xs[s][:, :, :], xs[s][:, :, :], bias[:, :].unsqueeze(1).to_broadcast([P, GROUP, D]),
                                   ALU.add).then_inc(bias_added[s], 1)

            def dst_diag_lo(i, s, a):
                pool.wait_ge(steps_done[s], steps_done.at(i, VECTOR_STEPS[3 * a] + 3))
                pool.tensor_tensor(dst_diag[s][:, 1, :, :], ident_h[:, :].unsqueeze(1).to_broadcast([P, GROUP, P]),
                                   dst_h[s][:, 1, :].unsqueeze(2).to_broadcast([P, GROUP, P]), ALU.mult).then_inc(diag_lo[s], 1)

            def probs_lo(i, s, a):
                pool.wait_ge(hi_part[s], hi_part.at(i, SPLIT[("probs0", "probs3")[a]] + 1))
                pool.wait_ge(full[s], full.at(i, SPLIT[("probs0", "probs3")[a]] + 1))
                pool.tensor_tensor(prob_lo[s][:, 0, 0:GROUP * P], prob[s][:, 0, 0:GROUP * P], prob_hi[s][:, 0, 0:GROUP * P],
                                   ALU.subtract).then_inc(lo_part[s], 1)

            def query_key_lo(i, s, j):
                pool.wait_ge(hi_part[s], hi_part.at(i, SPLIT["qk"] + j + 1))
                pool.wait_ge(full[s], full.at(i, SPLIT["qk"] + j + 1))
                pool.tensor_tensor(wide_lo[s][:, j, :], wide[s][:, j, :], wide_hi[s][:, j, :], ALU.subtract).then_inc(lo_part[s], 1)

            def heads_lo(i, s, b, k):
                pool.wait_ge(hi_part[s], hi_part.at(i, SPLIT["heads"] + BANKS * b + k + 1))
                pool.tensor_tensor(prob_lo[s][:, k, :], prob[s][:, k, :], prob_hi[s][:, k, :], ALU.subtract).then_inc(lo_part[s], 1)

            def slot(at):
                at(1, probs_lo, 0)
                at(3, heads_lo, 1, 1)
                at(2, query_key_lo, 1)
                at(2, query_key_lo, 2)
                at(2, query_key_lo, 3)
                at(1, norm_pow, 1)
                at(1, norm_shift, 1)
                at(1, split_lo, "h1")
                at(4, dst_diag_lo, 1)
                at(3, split_lo, "out")
                at(1, add_bias, 1, bias1)
                at(2, heads_lo, 0, 0)
                at(2, heads_lo, 0, 1)
                at(0, norm_pow, 0)
                at(4, probs_lo, 1)
                at(1, norm_pow, 2)
                at(0, norm_shift, 0)
                at(1, norm_shift, 2)
                at(1, split_lo, "h2")
                at(0, split_lo, "h0")
                at(1, add_bias, 2, bias2)
                at(3, norm_pow, 3)
                at(3, norm_shift, 3)
                at(0, dst_diag_lo, 0)
                at(2, heads_lo, 1, 0)
                at(3, split_lo, "h3")
                at(1, query_key_lo, 0)
            run(pool, slot)


def kernel(x, adj, L0_gnn_W, L0_gnn_a, L1_gnn_W, L1_gnn_b, L2_gnn_Wq, L2_gnn_bq, L2_gnn_Wk, L2_gnn_bk,
           L2_gnn_Wv, L2_gnn_bv, L2_gnn_Wo, L2_gnn_bo, L3_gnn_W, L3_gnn_a_src, L3_gnn_a_dst):
    import numpy as np
    import concourse.bacc as bacc
    from concourse.bass_utils import run_bass_kernel_spmd

    x, adj, w0, a0, w1, b1, wq, bq, wk, bk, wv, bv, wo, bo, w3, a_src, a_dst = (
        np.asarray(v) for v in (x, adj, L0_gnn_W, L0_gnn_a, L1_gnn_W, L1_gnn_b, L2_gnn_Wq, L2_gnn_bq, L2_gnn_Wk,
                                L2_gnn_bk, L2_gnn_Wv, L2_gnn_bv, L2_gnn_Wo, L2_gnn_bo, L3_gnn_W, L3_gnn_a_src,
                                L3_gnn_a_dst))
    columns = lambda v: v.reshape(-1, P).T
    arrays = {
        "in_x": x, "in_adj": adj, "in_adj_t": adj.T,
        "in_w0": w0, "in_w0_t": w0.T, "in_a0": a0[:, :, 0].T,
        "in_w_i": w1[:, :D].T, "in_w_j": w1[:, D:].T, "in_b1": b1,
        "in_w_q": wq.T, "in_w_k": wk.T, "in_b_qk": np.concatenate([columns(bq), columns(bk)], axis=1),
        "in_w_v": wv.T, "in_b_v": columns(bv), "in_w_o": wo.T, "in_b_o": bo,
        "in_w3": w3, "in_w3_t": w3.T, "in_a3": np.stack([a_src, a_dst], axis=1),
    }
    arrays = {k: np.ascontiguousarray(v) for k, v in arrays.items()}
    nc = bacc.Bacc("TRN2", target_bir_lowering=False, num_devices=1)
    args = [nc.dram_tensor(k, v.shape, mybir.dt.from_np(v.dtype), kind="ExternalInput").ap() for k, v in arrays.items()]
    out = nc.dram_tensor("out", x.shape, F32, kind="ExternalOutput").ap()
    nc.disable_value_cache = True
    build(nc, *args, out)
    return run_bass_kernel_spmd(nc, [arrays], core_ids=[0]).results[0]["out"]
```

```python
from contextlib import ExitStack

import concourse.bass as bass
from concourse import mybir

F32 = mybir.dt.float32
F16 = mybir.dt.float16
BF16 = mybir.dt.bfloat16
ALU = mybir.AluOpType
ACT = mybir.ActivationFunctionType
AX = mybir.AxisListType

P = 128
D = 256
KC = D // P
GROUP = 2
STREAMS = 4
HEADS = 8
DH = D // HEADS
QUADS = P // DH
BANKS = 2
BANK = 512
EPS = 1e-5
SLOPE = 0.2
MASKED = -1e30
WEIGHT_SCALE = 256.0
UNSCALE = 1.0 / WEIGHT_SCALE
F0 = 128
LAYERS = 4

COL_W0, COL_W3 = 0, F0 + 2
COL_WI = COL_W3 + D + 2
COL_WJ, COL_WQ, COL_WK, COL_WV, COL_WO = (COL_WI + D * k for k in range(1, 6))
COLS = COL_WO + D


X_UPDATES = [0, 1, 1 + GROUP, 1 + 2 * GROUP, 2 + 2 * GROUP]

VECTOR_STEPS = [0, 6, 6, 6 + GROUP, 12 + GROUP]
SPLIT = {"h0": 0, "probs0": GROUP, "h1": 1 + GROUP, "h2": 1 + 2 * GROUP, "qk": 1 + 3 * GROUP}
SPLIT |= {"heads": SPLIT["qk"] + 2 * KC, "out": SPLIT["qk"] + 2 * KC + BANKS}
HEAD_SPLITS = BANKS + 1
SPLIT |= {"h3": SPLIT["heads"] + HEAD_SPLITS * GROUP}
SPLIT |= {"probs3": SPLIT["h3"] + GROUP}
SPLITS = SPLIT["probs3"] + 1
PSUM_SPLIT = {"features0": 0, "aggregates": 1, "values": 1 + GROUP, "features3": 2 + GROUP}
FROM_PSUM = 3 + GROUP
TURN = {"h0": 0, "probs0": 1, "h2": 2, "heads": 3, "out": 3 + GROUP, "h3": 4 + GROUP, "probs3": 5 + GROUP}
TURNS = 6 + GROUP


def build(nc, x, adj, adj_t, w0, w0_t, a0, w_i, w_j, b1, w_q, w_k, b_qk, w_v, b_v, w_o, b_o, w3, w3_t, a3, out):
    graphs = x.shape[0]
    steps = graphs // (GROUP * STREAMS)
    assert graphs == steps * GROUP * STREAMS and x.shape[1] == P and x.shape[2] == D
    x_groups = x.rearrange("(g b) n d -> g n b d", b=GROUP)
    out_groups = out.rearrange("(g b) n d -> g n b d", b=GROUP)

    ctx = ExitStack()
    with ctx:
        def sb(name, shape, dt):
            return ctx.enter_context(nc.sbuf_tensor(name, shape, dt))

        def sem(name):
            return ctx.enter_context(nc.semaphore(name))

        def per_stream(name, shape, dt):
            return [sb(f"{name}{s}", shape, dt) for s in range(STREAMS)]

        adj_i = sb("adj_i", [P, 2, P], mybir.dt.int32)
        adj_f = sb("adj_f", [P, 2, P], F32)
        degree = sb("degree", [P, 1], F32)
        mask = sb("mask", [P, 2, P], BF16)
        agg_deg = sb("agg_deg", [P, 2 * P], F16)
        ident = sb("ident", [P, P], F32)
        ident_h = sb("ident_h", [P, P], F16)
        ident_b = sb("ident_b", [P, P], BF16)
        ones_h = sb("ones_h", [P, P], F16)
        minus_half = sb("minus_half", [P, GROUP], F32)
        w_f = sb("w_f", [P, KC, COLS], F32)
        w_hi = sb("w_hi", [P, KC, COLS], F16)
        w_lo = sb("w_lo", [P, KC, COLS], F16)
        w0t_f = sb("w0t_f", [P, D], F32)
        w3t_f = sb("w3t_f", [P, KC, D], F32)
        a0_f = sb("a0_f", [P, 2], F32)
        a3_f = sb("a3_f", [P, KC, 2], F32)
        bqk = sb("bqk", [P, 2 * KC], F32)
        bv_col = sb("bv_col", [P, KC], F32)
        bv_wide = sb("bv_wide", [P, KC, P], F32)
        b1_row = sb("b1_row", [P, D], F32)
        bo_row = sb("bo_row", [P, D], F32)
        bias = sb("bias", [P, 2, D], F32)
        bias_hi = sb("bias_hi", [P, 2, D], F16)
        bias_lo = sb("bias_lo", [P, 2, D], F16)

        x_in = per_stream("x_in", [P, GROUP, D], F32)
        xs = per_stream("xs", [P, GROUP, D], F32)
        y = per_stream("y", [P, GROUP, D], F32)
        stats = per_stream("stats", [P, GROUP, 6], F32)
        minus_mean = per_stream("minus_mean", [P, GROUP], F32)
        var = per_stream("var", [P, GROUP], F32)
        squares = per_stream("squares", [P, GROUP], F32)
        gap = per_stream("gap", [P, GROUP], F32)
        rstd = per_stream("rstd", [P, GROUP], F32)
        shift = per_stream("shift", [P, GROUP], F32)
        h_nat = per_stream("h_nat", [P, GROUP, D], F32)
        h_nat_hi = per_stream("h_nat_hi", [P, GROUP, D], F16)
        h_nat_lo = per_stream("h_nat_lo", [P, GROUP, D], F16)
        turned = per_stream("turned", [P, 2, KC, GROUP * P], F16)
        g_hi = [per_stream("g0_hi", [P, GROUP, F0 + 1], F16), per_stream("g3_hi", [P, GROUP, D + 1], F16)]
        g_lo = [per_stream("g0_lo", [P, GROUP, F0 + 1], F16), per_stream("g3_lo", [P, GROUP, D + 1], F16)]
        src_dst = per_stream("src_dst", [P, GROUP, 2], F32)
        dst_h = per_stream("dst_h", [P, 2, GROUP], F16)
        dst_diag = per_stream("dst_diag", [P, 2, GROUP, P], F16)
        logit_sum = per_stream("logit_sum", [P, GROUP, P], F32)
        logit = per_stream("logit", [P, GROUP, P], F32)
        minus_max = per_stream("minus_max", [P, GROUP], F32)
        sum_inverse = per_stream("sum_inverse", [P, GROUP], F32)
        wide = per_stream("wide", [P, 2 * KC, GROUP * P], F32)
        wide_hi = per_stream("wide_hi", [P, 2 * KC, GROUP * P], F16)
        wide_lo = per_stream("wide_lo", [P, 2 * KC, GROUP * P], F16)
        agg_h, agg_l = ([t[:, :, :].rearrange("p (b k) n -> p b (k n)", b=GROUP) for t in w] for w in (wide_hi, wide_lo))
        prob = per_stream("prob", [P, BANKS, BANK], F32)
        prob_hi = per_stream("prob_hi", [P, BANKS, BANK], F16)
        prob_lo = per_stream("prob_lo", [P, BANKS, BANK], F16)
        prob_t = per_stream("prob_t", [P, BANKS, 2, BANK], F16)
        v_hi = per_stream("v_hi", [P, GROUP, HEADS, DH + 1], F16)
        v_lo = per_stream("v_lo", [P, GROUP, HEADS, DH + 1], F16)
        heads_minus_max = per_stream("heads_minus_max", [P, BANKS, HEADS // BANKS], F32)
        heads_inverse = per_stream("heads_inverse", [P, HEADS], F32)

        ps = [ctx.enter_context(nc.psum_tensor(f"ps{s}", [P, BANKS, BANK], F32)) for s in range(STREAMS)]
        ps_h = [ps[s][:, :, :].bitcast(F16) for s in range(STREAMS)]

        def qk_out(s, j):
            return ps[s][:, j // KC, (j % KC) * GROUP * P:(j % KC + 1) * GROUP * P]

        constants_loaded = sem("constants_loaded")
        ident_ready = sem("ident_ready")
        setup = sem("setup_steps")
        setup_pe = sem("setup_products")
        weights_hi = sem("weights_hi")
        const_done = sem("constants_ready")

        class Signal:

            def __init__(self, name, per_step, start=0):
                self.sem = [sem(f"{name}{s}") for s in range(STREAMS)]
                self.per_step = per_step
                self.start = start

            def __getitem__(self, s):
                return self.sem[s]

            def at(self, i, k):
                return self.start + i * self.per_step + k

        loaded = Signal("loaded", 16)
        stored = Signal("stored", 16, start=16)
        steps_done = Signal("vector_steps", VECTOR_STEPS[LAYERS])
        norm_steps = Signal("norm_steps", 3 * LAYERS)
        moments = Signal("moments", LAYERS)
        norm_scale = Signal("norm_scale", LAYERS)
        norm_ready = Signal("norm_ready", LAYERS)
        full = Signal("full", SPLITS)
        hi_part = Signal("hi_part", SPLITS)
        lo_part = Signal("lo_part", SPLITS)
        psum_hi = Signal("psum_hi", FROM_PSUM)
        psum_lo = Signal("psum_lo", FROM_PSUM)
        turned_a = Signal("turned_a", TURNS)
        turned_b = Signal("turned_b", TURNS)
        copied_a = Signal("copied_a", TURNS)
        copied_b = Signal("copied_b", TURNS)
        x_updated = Signal("x_updated", X_UPDATES[LAYERS], start=1)
        g_made = Signal("gat_features", 2)
        diag_hi = Signal("diag_hi", 2)
        diag_lo = Signal("diag_lo", 2)
        dst_rows = Signal("dst_rows", 2)
        logits = Signal("logits", 2)
        g_out = Signal("gat_out", 2)
        agg = Signal("aggregated", GROUP)
        update = Signal("update", 2 * GROUP)
        qk = Signal("query_key", 2 * KC)
        v_made = Signal("values", GROUP)
        scores = Signal("scores", GROUP)
        half_scores = Signal("half_scores", GROUP)
        row_max = Signal("row_max", BANKS * GROUP)
        heads_out = Signal("heads_out", GROUP)

        both = range(STREAMS)

        def split_of(what, b):
            return SPLIT[what] + (HEAD_SPLITS if what == "out" else 1) * b

        def run(eng, slot):
            def slots(i, first=False, last=False):
                for r in range(STREAMS):
                    def at(part, piece, *which):
                        if not (first and part > r) and not (last and part <= r):
                            piece(i if part <= r else i - 1, (r - part) % STREAMS, *which)
                    slot(at)

            slots(0, first=True)
            with eng.Fori(1, steps) as i:
                slots(i)
            slots(steps, last=True)

        block = ctx.enter_context(nc.Block())

        @block.sync
        def _(sp):
            for dst, src in (
                (adj_i[:, 0, :], adj), (adj_i[:, 1, :], adj_t),
                (w_f[:, :, COL_W0:COL_W0 + F0], w0.rearrange("(c p) n -> p c n", p=P)),
                (w_f[:, :, COL_W3:COL_W3 + D], w3.rearrange("(c p) n -> p c n", p=P)),
                (w_f[:, :, COL_WI:COL_WI + D], w_i.rearrange("(c p) n -> p c n", p=P)),
                (w_f[:, :, COL_WJ:COL_WJ + D], w_j.rearrange("(c p) n -> p c n", p=P)),
                (w_f[:, :, COL_WQ:COL_WQ + D], w_q.rearrange("(c p) n -> p c n", p=P)),
                (w_f[:, :, COL_WK:COL_WK + D], w_k.rearrange("(c p) n -> p c n", p=P)),
                (w_f[:, :, COL_WV:COL_WV + D], w_v.rearrange("(c p) n -> p c n", p=P)),
                (w_f[:, :, COL_WO:COL_WO + D], w_o.rearrange("(c p) n -> p c n", p=P)),
                (w0t_f[:, :], w0_t), (w3t_f[:, :, :], w3_t.rearrange("(c p) n -> p c n", p=P)),
                (a0_f[:, :], a0), (a3_f[:, :, :], a3.rearrange("(c p) k -> p c k", p=P)),
                (bqk[:, :], b_qk), (bv_col[:, :], b_v),
                (b1_row[:, :], b1.partition_broadcast(P)), (bo_row[:, :], b_o.partition_broadcast(P)),
            ):
                sp.dma_start(dst, src).then_inc(constants_loaded, 16)
            for s in both:
                sp.dma_start(x_in[s][:, :, :], x_groups[s]).then_inc(loaded[s], 16)
            with sp.Fori(1, steps) as i:
                for s in both:
                    sp.wait_ge(x_updated[s], x_updated.at(i - 1, 1))
                    sp.dma_start(x_in[s][:, :, :], x_groups[i * STREAMS + s]).then_inc(loaded[s], 16)
            for s in both:
                sp.wait_ge(stored[s], stored.at(steps - 1, 16))

        n_loads = 18 * 16
        loaded_columns = [slice(COL_W0, COL_W0 + F0), slice(COL_W3, COL_W3 + D), slice(COL_WI, COLS)]

        @block.tensor
        def _(pe):
            pe.wait_ge(constants_loaded, n_loads)
            pe.wait_ge(setup, 2)
            for c in range(KC):
                pe.matmul(ps[0][:, 0, 2 * c:2 * c + 2], w0t_f[:, c * P:(c + 1) * P], a0_f[:, :], start=True, stop=True)
            for c in range(KC):
                for e in range(KC):
                    pe.matmul(ps[0][:, 1, 2 * c:2 * c + 2], w3t_f[:, e, c * P:(c + 1) * P], a3_f[:, e, :],
                              start=(e == 0), stop=(e == KC - 1))
            for c in range(KC):
                last = pe.matmul(ps[1][:, 0, 0:D], bv_wide[:, c, :], w_f[:, c, COL_WO:COL_WO + D],
                                 start=(c == 0), stop=(c == KC - 1))
            last.then_inc(setup_pe, 1)
            pe.wait_ge(const_done, 1)

            def product(out_ap, left, right, start=True, stop=True):
                for c in range(KC):
                    (lh, ll), (rh, rl) = left(c), right(c)
                    pe.matmul(out_ap, lh, rh, start=start and c == 0, stop=False)
                    pe.matmul(out_ap, lh, rl, start=False, stop=False)
                    last = pe.matmul(out_ap, ll, rh, start=False, stop=stop and c == KC - 1)
                return last

            def weights(col, n):
                return lambda c: (w_hi[:, c, col:col + n], w_lo[:, c, col:col + n])

            def turned_cols(s, b, n):
                return lambda c: (turned[s][:, 0, c, b * P:b * P + n], turned[s][:, 1, c, b * P:b * P + n])

            def turn(i, s, b, half):
                src, done = ((h_nat_hi, turned_a), (h_nat_lo, turned_b))[half]
                for c in range(KC):
                    last = pe.transpose(ps_h[s][:, half, (c * GROUP + b) * P:(c * GROUP + b + 1) * P],
                                        src[s][:, b, c * P:(c + 1) * P], ident_h[:, :])
                if b == GROUP - 1:
                    last.then_inc(done[s], 1)

            def turn_hi(i, s, what, b):
                if what == "h0" and b == 0:
                    pe.wait_ge(x_updated[s], x_updated.at(i, 0))
                pe.wait_ge(hi_part[s], hi_part.at(i, SPLIT[what] + b + 1))
                turn(i, s, b, 0)

            def turn_lo(i, s, what, b):
                pe.wait_ge(lo_part[s], lo_part.at(i, SPLIT[what] + b + 1))
                turn(i, s, b, 1)

            def turn_out(i, s, half):
                part = (hi_part, lo_part)[half]
                pe.wait_ge(part[s], part.at(i, SPLIT["out"] + HEAD_SPLITS * (GROUP - 1) + 1))
                for b in range(GROUP):
                    turn(i, s, b, half)

            def wait_turned(i, s, what):
                pe.wait_ge(copied_a[s], copied_a.at(i, TURN[what] + 1))
                pe.wait_ge(copied_b[s], copied_b.at(i, TURN[what] + 1))

            def features(i, s, a):
                f, col = (F0, COL_W0) if a == 0 else (D, COL_W3)
                wait_turned(i, s, ("h0", "h3")[a])
                for b in range(GROUP):
                    last = product(ps[s][:, b, 0:f + 2], turned_cols(s, b, P), weights(col, f + 2))
                last.then_inc(g_made[s], 1)

            def dst_rows_sum(i, s, a):
                pe.wait_ge(psum_lo[s], psum_lo.at(i, PSUM_SPLIT[("features0", "features3")[a]] + 1))
                pe.wait_ge(diag_hi[s], diag_hi.at(i, a + 1))
                pe.matmul(ps[s][:, 0, 0:GROUP * P], ident_b[:, :], mask[:, :, :].rearrange("p g j -> p (g j)"), start=True, stop=False)
                pe.matmul(ps[s][:, 0, 0:GROUP * P], ones_h[:, :], dst_diag[s][:, 0, :, :].rearrange("p g j -> p (g j)"),
                          start=False, stop=False)
                pe.wait_ge(diag_lo[s], diag_lo.at(i, a + 1))
                pe.matmul(ps[s][:, 0, 0:GROUP * P], ones_h[:, :], dst_diag[s][:, 1, :, :].rearrange("p g j -> p (g j)"),
                          start=False, stop=True).then_inc(dst_rows[s], 1)

            def turn_probs(i, s, a, half):
                part, src, done, bank = ((hi_part, prob_hi, turned_a, 1), (lo_part, prob_lo, turned_b, 0))[half]
                pe.wait_ge(part[s], part.at(i, SPLIT[("probs0", "probs3")[a]] + 1))
                for b in range(GROUP):
                    last = pe.transpose(ps_h[s][:, bank, b * P:(b + 1) * P], src[s][:, 0, b * P:(b + 1) * P], ident_h[:, :])
                last.then_inc(done[s], 1)

            def gat_sum(i, s, a):
                f = F0 if a == 0 else D
                wait_turned(i, s, ("probs0", "probs3")[a])
                for b in range(GROUP):
                    ph, pl = (prob_t[s][:, 0, k, b * P:(b + 1) * P] for k in range(2))
                    o = ps[s][:, b, 0:f + 1]
                    pe.matmul(o, ph, g_hi[a][s][:, b, :], start=True, stop=False)
                    pe.matmul(o, ph, g_lo[a][s][:, b, :], start=False, stop=False)
                    last = pe.matmul(o, pl, g_hi[a][s][:, b, :], start=False, stop=True)
                last.then_inc(g_out[s], 1)

            def aggregate(i, s, b):
                pe.wait_ge(hi_part[s], hi_part.at(i, SPLIT["h1"] + b + 1))
                pe.wait_ge(lo_part[s], lo_part.at(i, SPLIT["h1"] + b + 1))
                for c in range(KC):
                    o = ps[s][:, b, c * 2 * P:(c + 1) * 2 * P]
                    pe.matmul(o, h_nat_hi[s][:, b, c * P:(c + 1) * P], agg_deg[:, :], start=True, stop=False)
                    last = pe.matmul(o, h_nat_lo[s][:, b, c * P:(c + 1) * P], agg_deg[:, :], start=False, stop=True)
                last.then_inc(agg[s], 1)

            def bias_product(out_ap, left, layer):
                pe.matmul(out_ap, left, bias_hi[:, layer, :], start=True, stop=False)
                pe.matmul(out_ap, left, bias_lo[:, layer, :], start=False, stop=False)

            def messages(i, s, b):
                pe.wait_ge(psum_hi[s], psum_hi.at(i, PSUM_SPLIT["aggregates"] + b + 1))
                pe.wait_ge(psum_lo[s], psum_lo.at(i, PSUM_SPLIT["aggregates"] + b + 1))
                bias_product(ps[s][:, b, 0:D], agg_deg[:, P:2 * P], 0)
                for part, col in ((0, COL_WJ), (1, COL_WI)):
                    def left(c):
                        at = slice(c * 2 * P + part * P, c * 2 * P + (part + 1) * P)
                        return agg_h[s][:, b, at], agg_l[s][:, b, at]
                    last = product(ps[s][:, b, 0:D], left, weights(col, D), start=False, stop=(part == 1))
                last.then_inc(update[s], 1)

            def query_key(i, s, j):
                wait_turned(i, s, "h2")
                col = (COL_WQ, COL_WK)[j // KC] + (j % KC) * P
                product(qk_out(s, j), weights(col, P), turned_cols(s, 0, GROUP * P)).then_inc(qk[s], 1)

            def values(i, s, b):
                pe.wait_ge(full[s], full.at(i, SPLIT["qk"] + KC))
                product(ps[s][:, 0, b * D:(b + 1) * D], turned_cols(s, b, P), weights(COL_WV, D)).then_inc(v_made[s], 1)

            def head_scores(i, s, b, half):
                if half == 0 and b == 0:
                    pe.wait_ge(hi_part[s], hi_part.at(i, SPLIT["qk"] + 2 * KC))
                    pe.wait_ge(lo_part[s], lo_part.at(i, SPLIT["qk"] + 2 * KC))
                    pe.wait_ge(psum_hi[s], psum_hi.at(i, PSUM_SPLIT["values"] + 1))
                    pe.wait_ge(psum_lo[s], psum_lo.at(i, PSUM_SPLIT["values"] + 1))
                elif half == 0:
                    pe.wait_ge(full[s], full.at(i, SPLIT["out"] + HEAD_SPLITS * (b - 1) + 1))
                for k in range(BANKS):
                    pe.matmul(ps[s][:, k, half * KC * P:(half + 1) * KC * P], ident_b[:, :],
                              mask[:, :, :].rearrange("p g j -> p (g j)"), start=True, stop=False)
                if half == 1:
                    pe.wait_ge(half_scores[s], half_scores.at(i, b + 1))
                for c in range(KC):
                    for t, (q, kk) in enumerate(((wide_hi, wide_hi), (wide_hi, wide_lo), (wide_lo, wide_hi))):
                        for k in range(BANKS):
                            a = half * BANKS + k
                            rows = slice(a * DH, (a + 1) * DH)
                            last = pe.matmul(ps[s][:, k, (half * KC + c) * P:(half * KC + c + 1) * P],
                                             q[s][rows, c, b * P:(b + 1) * P], kk[s][rows, KC + c, b * P:(b + 1) * P],
                                             start=False, stop=(t == 2 and c == KC - 1))
                last.then_inc((half_scores, scores)[half][s], 1)

            def turn_heads(i, s, b, k):
                pe.wait_ge(hi_part[s], hi_part.at(i, SPLIT["heads"] + HEAD_SPLITS * b + k + 1))
                pe.wait_ge(lo_part[s], lo_part.at(i, SPLIT["heads"] + HEAD_SPLITS * b + k + 1))
                for part, src in enumerate((prob_hi, prob_lo)):
                    for j in range(BANK // P):
                        last = pe.transpose(ps_h[s][:, k, part * BANK + j * P:part * BANK + (j + 1) * P],
                                            src[s][:, k, j * P:(j + 1) * P], ident_h[:, :])
                last.then_inc((turned_a, turned_b)[k][s], 1)

            def sum_heads(i, s, b):
                pe.wait_ge(copied_a[s], copied_a.at(i, TURN["heads"] + b + 1))
                pe.wait_ge(copied_b[s], copied_b.at(i, TURN["heads"] + b + 1))
                for h in range(HEADS):
                    c, a = h // QUADS, h % QUADS
                    o = ps[s][:, 0, h * (DH + 1):(h + 1) * (DH + 1)]
                    col = ((a // BANKS) * KC + c) * P
                    ph, pl = (prob_t[s][:, a % BANKS, part, col:col + P] for part in range(2))
                    pe.matmul(o, ph, v_hi[s][:, b, h, :], start=True, stop=False)
                    pe.matmul(o, ph, v_lo[s][:, b, h, :], start=False, stop=False)
                    last = pe.matmul(o, pl, v_hi[s][:, b, h, :], start=False, stop=True)
                last.then_inc(heads_out[s], 1)

            def project(i, s, b):
                wait_turned(i, s, "out")
                bias_product(ps[s][:, b, 0:D], ident_h[:, :], 1)
                product(ps[s][:, b, 0:D], turned_cols(s, b, P), weights(COL_WO, D), start=False).then_inc(update[s], 1)

            def slot(at):
                at(2, values, 0)
                at(2, values, 1)
                at(3, turn_heads, 1, 0)
                at(3, turn_heads, 1, 1)
                at(4, dst_rows_sum, 1)
                at(3, sum_heads, 1)
                at(2, head_scores, 0, 0)
                at(1, aggregate, 0)
                at(3, turn_out, 0)
                at(4, turn_probs, 1, 0)
                at(2, head_scores, 0, 1)
                at(1, aggregate, 1)
                at(4, turn_probs, 1, 1)
                at(1, messages, 0)
                at(4, gat_sum, 1)
                at(3, turn_out, 1)
                at(1, messages, 1)
                at(0, turn_hi, "h0", 0)
                at(0, turn_hi, "h0", 1)
                at(3, project, 0)
                at(3, project, 1)
                at(0, turn_lo, "h0", 0)
                at(0, turn_lo, "h0", 1)
                at(2, turn_heads, 0, 0)
                at(2, turn_heads, 0, 1)
                at(0, features, 0)
                at(2, sum_heads, 0)
                at(0, dst_rows_sum, 0)
                at(1, turn_hi, "h2", 0)
                at(2, head_scores, 1, 0)
                at(1, turn_lo, "h2", 0)
                at(1, turn_hi, "h2", 1)
                at(2, head_scores, 1, 1)
                at(1, turn_lo, "h2", 1)
                at(3, turn_hi, "h3", 0)
                at(3, turn_lo, "h3", 0)
                at(0, turn_probs, 0, 0)
                at(3, turn_hi, "h3", 1)
                at(1, query_key, 0)
                at(0, turn_probs, 0, 1)
                at(1, query_key, 1)
                at(0, gat_sum, 0)
                at(3, turn_lo, "h3", 1)
                at(1, query_key, 2)
                at(1, query_key, 3)
                at(3, features, 1)
            run(pe, slot)

        @block.vector
        def _(dve):
            dve.wait_ge(constants_loaded, n_loads)
            n = 0

            def link(ins):
                nonlocal n
                ins.then_inc(setup, 1)
                n += 1
                dve.wait_ge(setup, n)

            for s in both:
                dve.memset(y[s][:, :, :], 0.0).then_inc(stored[s], 16)
                dve.memset(xs[s][:, :, :], 0.0).then_inc(x_updated[s], 1)
            link(dve.memset(bv_wide[:, :, :], 0.0))
            for c in range(KC):
                last = dve.tensor_scalar(bv_wide[:, c, :], bv_wide[:, c, :], bv_col[:, c:c + 1], None, ALU.add)
            link(last)
            link(dve.tensor_copy(adj_f[:, :, :], adj_i[:, :, :]))
            dve.tensor_copy(agg_deg[:, 0:P], adj_f[:, 1, :])
            for g in range(2):
                dve.tensor_scalar(mask[:, g, :], adj_f[:, 0, :], -1.0, -MASKED, ALU.add, ALU.mult)
            link(dve.tensor_reduce(degree[:, :], adj_f[:, 0, :], AX.X, ALU.add))
            dve.tensor_copy(bias[:, 0, :], b1_row[:, :])
            dve.memset(minus_half[:, :], -0.5)
            dve.memset(ones_h[:, :], 1.0)
            for s in both:
                dve.memset(g_hi[0][s][:, :, F0:F0 + 1], 1.0)
                dve.memset(g_hi[1][s][:, :, D:D + 1], 1.0)
                dve.memset(g_lo[0][s][:, :, F0:F0 + 1], 0.0)
                dve.memset(g_lo[1][s][:, :, D:D + 1], 0.0)
                dve.memset(v_hi[s][:, :, :, DH:DH + 1], 1.0)
                dve.memset(v_lo[s][:, :, :, DH:DH + 1], 0.0)
            dve.tensor_scalar(bqk[:, 0:KC], bqk[:, 0:KC], float(DH) ** -0.5, None, ALU.mult)
            dve.wait_ge(weights_hi, 1)
            for cols in loaded_columns:
                dve.scalar_tensor_tensor(w_lo[:, :, cols], w_f[:, :, cols], WEIGHT_SCALE, w_hi[:, :, cols], ALU.mult, ALU.subtract)
            dve.wait_ge(setup_pe, 1)
            made = [slice(COL_W0 + F0, COL_W0 + F0 + 2), slice(COL_W3 + D, COL_W3 + D + 2)]
            for bank, cols in enumerate(made):
                dve.tensor_scalar(w_f[:, :, cols], ps[0][:, bank, 0:2 * KC].rearrange("p (c k) -> p c k", c=KC), WEIGHT_SCALE, None,
                                  ALU.mult)
            link(dve.tensor_tensor(bias[:, 1, :], ps[1][:, 0, 0:D], bo_row[:, :], ALU.add))
            link(dve.tensor_scalar(bias[:, :, :], bias[:, :, :], WEIGHT_SCALE, None, ALU.mult))
            for cols in made:
                dve.tensor_copy(w_hi[:, :, cols], w_f[:, :, cols])
            link(dve.tensor_copy(bias_hi[:, :, :], bias[:, :, :]))
            for cols in made:
                dve.tensor_tensor(w_lo[:, :, cols], w_f[:, :, cols], w_hi[:, :, cols], ALU.subtract)
            dve.tensor_tensor(bias_lo[:, :, :], bias[:, :, :], bias_hi[:, :, :], ALU.subtract)
            dve.wait_ge(ident_ready, 2)
            dve.tensor_copy(ident_h[:, :], ident[:, :])
            dve.tensor_copy(ident_b[:, :], ident[:, :])
            dve.tensor_scalar(agg_deg[:, P:2 * P], ident[:, :], degree[:, 0:1], None, ALU.mult).then_inc(const_done, 1)
            dve.wait_ge(const_done, 1)

            def norm_stats(i, s, l, b):
                if l == 0:
                    dve.wait_ge(loaded[s], loaded.at(i, 16))
                elif l == 1:
                    dve.wait_ge(x_updated[s], x_updated.at(i, X_UPDATES[1]))
                else:
                    dve.wait_ge(x_updated[s], x_updated.at(i, X_UPDATES[l - 1] + b + 1))
                last = dve.bn_stats(stats[s][:, b, :], (x_in if l == 0 else xs)[s][:, b, :])
                if b == GROUP - 1:
                    last.then_inc(norm_steps[s], 1)

            def moments_a(i, s, l):
                even, odd = stats[s][:, :, 0:3], stats[s][:, :, 3:6]
                dve.wait_ge(norm_steps[s], norm_steps.at(i, 3 * l + 1))
                dve.tensor_tensor(gap[s][:, :], even[:, :, 1], odd[:, :, 1], ALU.subtract)
                dve.tensor_tensor(minus_mean[s][:, :], even[:, :, 1], odd[:, :, 1], ALU.add)
                dve.tensor_tensor(squares[s][:, :], even[:, :, 2], odd[:, :, 2], ALU.add).then_inc(norm_steps[s], 1)

            def moments_b(i, s, l):
                dve.wait_ge(norm_steps[s], norm_steps.at(i, 3 * l + 2))
                dve.scalar_tensor_tensor(gap[s][:, :], gap[s][:, :], 0.25, gap[s][:, :], ALU.mult, ALU.mult)
                dve.tensor_scalar(squares[s][:, :], squares[s][:, :], 1.0 / D, EPS, ALU.mult, ALU.add)
                dve.tensor_scalar(minus_mean[s][:, :], minus_mean[s][:, :], -0.5, None, ALU.mult).then_inc(norm_steps[s], 1)

            def moments_c(i, s, l):
                dve.wait_ge(norm_steps[s], norm_steps.at(i, 3 * l + 3))
                dve.tensor_tensor(var[s][:, :], squares[s][:, :], gap[s][:, :], ALU.add).then_inc(moments[s], 1)

            def split_hi(i, s, what, b):
                dve.wait_ge(full[s], full.at(i, split_of(what, b) + 1))
                dve.tensor_copy(h_nat_hi[s][:, b, :], h_nat[s][:, b, :]).then_inc(hi_part[s], 1)

            def copy_turned_hi(i, s, what):
                dve.wait_ge(turned_a[s], turned_a.at(i, TURN[what] + 1))
                dve.tensor_copy(turned[s][:, 0, :, :].rearrange("p c n -> p (c n)"), ps_h[s][:, 0, 0:KC * GROUP * P])\
                   .then_inc(copied_a[s], 1)

            def dst_cols(i, s, a):
                f = F0 if a == 0 else D
                dve.wait_ge(g_made[s], g_made.at(i, a + 1))
                dve.tensor_scalar(src_dst[s][:, :, :], ps[s][:, :, f:f + 2], UNSCALE, None, ALU.mult).then_inc(steps_done[s], 1)
                dve.tensor_scalar(dst_h[s][:, 0, :], ps[s][:, :, f + 1], UNSCALE, None, ALU.mult).then_inc(steps_done[s], 1)

            def dst_lo(i, s, a):
                dve.wait_ge(steps_done[s], steps_done.at(i, VECTOR_STEPS[3 * a] + 2))
                dve.tensor_tensor(dst_h[s][:, 1, :], src_dst[s][:, :, 1], dst_h[s][:, 0, :], ALU.subtract).then_inc(steps_done[s], 1)
                dve.tensor_tensor(dst_diag[s][:, 0, :, :], ident_h[:, :].unsqueeze(1).to_broadcast([P, GROUP, P]),
                                  dst_h[s][:, 0, :].unsqueeze(2).to_broadcast([P, GROUP, P]), ALU.mult).then_inc(diag_hi[s], 1)

            def features_lo(i, s, a):
                f = F0 if a == 0 else D
                dve.wait_ge(psum_hi[s], psum_hi.at(i, PSUM_SPLIT[("features0", "features3")[a]] + 1))
                last = dve.scalar_tensor_tensor(g_lo[a][s][:, :, 0:f], ps[s][:, :, 0:f], UNSCALE, g_hi[a][s][:, :, 0:f],
                                                ALU.mult, ALU.subtract)
                if a == 0:
                    last = dve.scalar_tensor_tensor(xs[s][:, :, F0:D], ps[s][:, :, 0:F0], UNSCALE, x_in[s][:, :, F0:D],
                                                    ALU.mult, ALU.add)
                last.then_inc(psum_lo[s], 1)

            def logits_sum(i, s, a):
                dve.wait_ge(dst_rows[s], dst_rows.at(i, a + 1))
                dve.tensor_tensor(logit_sum[s][:, :, :], ps[s][:, 0, 0:GROUP * P].rearrange("p (g j) -> p g j", g=GROUP),
                                  src_dst[s][:, :, 0:1].to_broadcast([P, GROUP, P]), ALU.add).then_inc(steps_done[s], 1)

            def logits_leaky(i, s, a):
                dve.wait_ge(steps_done[s], steps_done.at(i, VECTOR_STEPS[3 * a] + 4))
                dve.scalar_tensor_tensor(logit[s][:, :, :], logit_sum[s][:, :, :], SLOPE, logit_sum[s][:, :, :], ALU.mult, ALU.max)\
                   .then_inc(steps_done[s], 1)

            def logits_max(i, s, a):
                dve.wait_ge(steps_done[s], steps_done.at(i, VECTOR_STEPS[3 * a] + 5))
                dve.tensor_reduce(minus_max[s][:, :], logit[s][:, :, :], AX.X, ALU.max, negate=True).then_inc(logits[s], 1)

            def copy_probs(i, s, a):
                dve.wait_ge(turned_a[s], turned_a.at(i, TURN[("probs0", "probs3")[a]] + 1))
                dve.tensor_copy(prob_t[s][:, 0, 0, 0:GROUP * P], ps_h[s][:, 1, 0:GROUP * P]).then_inc(copied_a[s], 1)

            def invert_sums(i, s, a):
                dve.wait_ge(g_out[s], g_out.at(i, a + 1))
                dve.reciprocal(sum_inverse[s][:, :], ps[s][:, :, F0 if a == 0 else D]).then_inc(steps_done[s], 1)

            def gat_residual(i, s, a):
                f = F0 if a == 0 else D
                dve.wait_ge(steps_done[s], steps_done.at(i, VECTOR_STEPS[3 * a] + 6))
                if a == 1:
                    dve.wait_ge(stored[s], stored.at(i, 0))
                old, new = ((x_in, xs) if a == 0 else (xs, y))
                for b in range(GROUP):
                    last = dve.scalar_tensor_tensor(new[s][:, b, 0:f], ps[s][:, b, 0:f], sum_inverse[s][:, b:b + 1], old[s][:, b, 0:f],
                                                    ALU.mult, ALU.add)
                last.then_inc(x_updated[s], 1)

            def aggregates_lo(i, s, b):
                dve.wait_ge(psum_hi[s], psum_hi.at(i, PSUM_SPLIT["aggregates"] + b + 1))
                dve.tensor_tensor(agg_l[s][:, b, :], ps[s][:, b, :], agg_h[s][:, b, :], ALU.subtract).then_inc(psum_lo[s], 1)

            def linear_residual(i, s, l, b):
                dve.wait_ge(update[s], update.at(i, (l - 1) * GROUP + b + 1))
                dve.scalar_tensor_tensor(xs[s][:, b, :], ps[s][:, b, 0:D], UNSCALE, xs[s][:, b, :], ALU.mult, ALU.add)\
                   .then_inc(x_updated[s], 1)

            def values_lo(i, s):
                dve.wait_ge(psum_hi[s], psum_hi.at(i, PSUM_SPLIT["values"] + 1))
                for b in range(GROUP):
                    last = dve.scalar_tensor_tensor(v_lo[s][:, b, :, 0:DH],
                                                    ps[s][:, 0, b * D:(b + 1) * D].rearrange("p (h d) -> p h d", h=HEADS),
                                                    UNSCALE, v_hi[s][:, b, :, 0:DH], ALU.mult, ALU.subtract)
                last.then_inc(psum_lo[s], 1)

            def heads_max(i, s, b, k):
                dve.wait_ge(scores[s], scores.at(i, b + 1))
                dve.tensor_reduce(heads_minus_max[s][:, k, :], ps[s][:, k, :].rearrange("p (j k) -> p j k", k=P), AX.X, ALU.max,
                                  negate=True).then_inc(row_max[s], 1)

            def heads_hi(i, s, b, k):
                dve.wait_ge(full[s], full.at(i, SPLIT["heads"] + HEAD_SPLITS * b + k + 1))
                dve.tensor_copy(prob_hi[s][:, k, :], prob[s][:, k, :]).then_inc(hi_part[s], 1)

            def copy_heads(i, s, b):
                dve.wait_ge(turned_a[s], turned_a.at(i, TURN["heads"] + b + 1))
                dve.tensor_copy(prob_t[s][:, 0, :, :].rearrange("p k n -> p (k n)"), ps_h[s][:, 0, :]).then_inc(copied_a[s], 1)

            def head_cols(s):
                return ps[s][:, 0, 0:HEADS * (DH + 1)].rearrange("p (h d) -> p h d", h=HEADS)

            def invert_heads(i, s, b):
                dve.wait_ge(heads_out[s], heads_out.at(i, b + 1))
                dve.reciprocal(heads_inverse[s][:, :], head_cols(s)[:, :, DH]).then_inc(steps_done[s], 1)

            def normalise(i, s, b):
                dve.wait_ge(steps_done[s], steps_done.at(i, VECTOR_STEPS[2] + b + 1))
                dve.tensor_tensor(h_nat[s][:, b, :].rearrange("p (h d) -> p h d", h=HEADS), head_cols(s)[:, :, 0:DH],
                                  heads_inverse[s][:, :].unsqueeze(2).to_broadcast([P, HEADS, DH]), ALU.mult)\
                   .then_inc(full[s], 1)

            def slot(at):
                at(3, heads_hi, 1, 1)
                at(1, norm_stats, 1, 0)
                at(0, norm_stats, 0, 0)
                at(1, norm_stats, 1, 1)
                at(0, norm_stats, 0, 1)
                at(1, moments_a, 1)
                at(0, moments_a, 0)
                at(4, dst_cols, 1)
                at(1, moments_b, 1)
                at(4, dst_lo, 1)
                at(1, moments_c, 1)
                at(0, moments_b, 0)
                at(4, features_lo, 1)
                at(0, moments_c, 0)
                at(3, copy_heads, 1)
                at(2, values_lo)
                at(4, logits_sum, 1)
                at(4, logits_leaky, 1)
                at(1, split_hi, "h1", 0)
                at(4, logits_max, 1)
                at(3, invert_heads, 1)
                at(3, normalise, 1)
                at(3, split_hi, "out", 1)
                at(1, split_hi, "h1", 1)
                at(3, copy_turned_hi, "out")
                at(1, aggregates_lo, 0)
                at(0, split_hi, "h0", 0)
                at(2, heads_max, 0, 0)
                at(4, copy_probs, 1)
                at(2, heads_max, 0, 1)
                at(1, aggregates_lo, 1)
                at(0, split_hi, "h0", 1)
                at(2, heads_hi, 0, 0)
                at(4, invert_sums, 1)
                at(1, linear_residual, 1, 0)
                at(4, gat_residual, 1)
                at(2, heads_hi, 0, 1)
                at(1, norm_stats, 2, 0)
                at(1, linear_residual, 1, 1)
                at(0, copy_turned_hi, "h0")
                at(1, norm_stats, 2, 1)
                at(3, linear_residual, 2, 0)
                at(1, moments_a, 2)
                at(3, norm_stats, 3, 0)
                at(3, linear_residual, 2, 1)
                at(1, moments_b, 2)
                at(3, norm_stats, 3, 1)
                at(1, moments_c, 2)
                at(2, copy_heads, 0)
                at(3, moments_a, 3)
                at(0, dst_cols, 0)
                at(3, moments_b, 3)
                at(0, dst_lo, 0)
                at(3, moments_c, 3)
                at(0, features_lo, 0)
                at(2, invert_heads, 0)
                at(1, split_hi, "h2", 0)
                at(2, normalise, 0)
                at(0, logits_sum, 0)
                at(1, split_hi, "h2", 1)
                at(0, logits_leaky, 0)
                at(0, logits_max, 0)
                at(3, split_hi, "h3", 0)
                at(3, split_hi, "h3", 1)
                at(1, copy_turned_hi, "h2")
                at(2, heads_max, 1, 0)
                at(2, split_hi, "out", 0)
                at(2, heads_max, 1, 1)
                at(0, copy_probs, 0)
                at(2, heads_hi, 1, 0)
                at(3, copy_turned_hi, "h3")
                at(0, invert_sums, 0)
                at(0, gat_residual, 0)
            run(dve, slot)

        @block.scalar
        def _(act):
            act.wait_ge(constants_loaded, n_loads)
            for cols in loaded_columns:
                last = act.activation(w_hi[:, :, cols], w_f[:, :, cols], ACT.Copy, scale=WEIGHT_SCALE)
            last.then_inc(weights_hi, 1)
            act.wait_ge(const_done, 1)

            def norm_apply(i, s, l, b):
                act.wait_ge(norm_ready[s], norm_ready.at(i, l + 1))
                act.activation(h_nat[s][:, b, :], (x_in if l == 0 else xs)[s][:, b, :], ACT.Relu, bias=shift[s][:, b:b + 1],
                               scale=rstd[s][:, b:b + 1]).then_inc(full[s], 1)

            def copy_turned_lo(i, s, what):
                act.wait_ge(turned_b[s], turned_b.at(i, TURN[what] + 1))
                act.activation(turned[s][:, 1, :, :].rearrange("p c n -> p (c n)"), ps_h[s][:, 1, 0:KC * GROUP * P], ACT.Copy)\
                   .then_inc(copied_b[s], 1)

            def features_hi(i, s, a):
                f = F0 if a == 0 else D
                act.wait_ge(steps_done[s], steps_done.at(i, VECTOR_STEPS[3 * a] + 2))
                act.activation(g_hi[a][s][:, :, 0:f], ps[s][:, :, 0:f], ACT.Copy, scale=UNSCALE).then_inc(psum_hi[s], 1)

            def gat_exp(i, s, a):
                act.wait_ge(logits[s], logits.at(i, a + 1))
                for dst, done in ((prob_hi, hi_part), (prob, full)):
                    for b in range(GROUP):
                        last = act.activation(dst[s][:, 0, b * P:(b + 1) * P], logit[s][:, b, :], ACT.Exp, bias=minus_max[s][:, b:b + 1])
                    last.then_inc(done[s], 1)

            def copy_probs_lo(i, s, a):
                act.wait_ge(turned_b[s], turned_b.at(i, TURN[("probs0", "probs3")[a]] + 1))
                act.activation(prob_t[s][:, 0, 1, 0:GROUP * P], ps_h[s][:, 0, 0:GROUP * P], ACT.Copy).then_inc(copied_b[s], 1)

            def aggregates_hi(i, s, b):
                act.wait_ge(agg[s], agg.at(i, b + 1))
                act.activation(agg_h[s][:, b, :], ps[s][:, b, :], ACT.Copy).then_inc(psum_hi[s], 1)

            def query_key_copy(i, s, j):
                act.wait_ge(qk[s], qk.at(i, (j // KC + 1) * KC))
                for dst, done in ((wide_hi, hi_part), (wide, full)):
                    act.activation(dst[s][:, j, :], qk_out(s, j), ACT.Identity, bias=bqk[:, j:j + 1],
                                   scale=UNSCALE * (float(DH) ** -0.5 if j < KC else 1.0)).then_inc(done[s], 1)

            def values_hi(i, s):
                act.wait_ge(v_made[s], v_made.at(i, GROUP))
                act.activation(v_hi[s][:, :, :, 0:DH], ps[s][:, 0, :].rearrange("p (g h d) -> p g h d", g=GROUP, h=HEADS), ACT.Copy,
                               scale=UNSCALE).then_inc(psum_hi[s], 1)

            def heads_exp(i, s, b, k):
                act.wait_ge(row_max[s], row_max.at(i, BANKS * b + k + 1))
                for j in range(BANK // P):
                    at = slice(j * P, (j + 1) * P)
                    last = act.activation(prob[s][:, k, at], ps[s][:, k, at], ACT.Exp, bias=heads_minus_max[s][:, k, j:j + 1])
                last.then_inc(full[s], 1)

            def copy_heads_1(i, s, b):
                act.wait_ge(turned_b[s], turned_b.at(i, TURN["heads"] + b + 1))
                act.activation(prob_t[s][:, 1, :, :].rearrange("p k n -> p (k n)"), ps_h[s][:, 1, :], ACT.Copy)\
                   .then_inc(copied_b[s], 1)

            def store(i, s):
                act.wait_ge(x_updated[s], x_updated.at(i, X_UPDATES[LAYERS]))
                act.dma_start(out_groups[i * STREAMS + s], y[s][:, :, :]).then_inc(stored[s], 16)

            def slot(at):
                at(2, query_key_copy, 1)
                at(2, query_key_copy, 2)
                at(4, features_hi, 1)
                at(2, query_key_copy, 3)
                at(2, values_hi)
                at(3, copy_heads_1, 1)
                at(1, norm_apply, 1, 0)
                at(1, norm_apply, 1, 1)
                at(4, gat_exp, 1)
                at(1, aggregates_hi, 0)
                at(0, norm_apply, 0, 0)
                at(0, norm_apply, 0, 1)
                at(1, aggregates_hi, 1)
                at(4, copy_probs_lo, 1)
                at(2, heads_exp, 0, 0)
                at(2, heads_exp, 0, 1)
                at(3, copy_turned_lo, "out")
                at(0, copy_turned_lo, "h0")
                at(2, copy_heads_1, 0)
                at(0, features_hi, 0)
                at(1, norm_apply, 2, 0)
                at(1, norm_apply, 2, 1)
                at(3, norm_apply, 3, 0)
                at(3, norm_apply, 3, 1)
                at(4, store)
                at(0, gat_exp, 0)
                at(1, copy_turned_lo, "h2")
                at(2, heads_exp, 1, 0)
                at(0, copy_probs_lo, 0)
                at(2, heads_exp, 1, 1)
                at(3, copy_turned_lo, "h3")
                at(1, query_key_copy, 0)
            run(act, slot)

        @block.gpsimd
        def _(pool):
            pool.memset(ident[:, :], 0.0).then_inc(ident_ready, 1)
            pool.wait_ge(ident_ready, 1)
            pool.affine_select(out=ident[:, :], in_=ident[:, :], compare_op=ALU.not_equal, fill=1.0, base=0,
                               pattern=[[-1, P]], channel_multiplier=1).then_inc(ident_ready, 1)
            pool.wait_ge(const_done, 1)

            def norm_pow(i, s, l):
                pool.wait_ge(moments[s], moments.at(i, l + 1))
                pool.tensor_tensor(rstd[s][:, :], var[s][:, :], minus_half[:, :], ALU.pow).then_inc(norm_scale[s], 1)

            def norm_shift(i, s, l):
                pool.wait_ge(norm_scale[s], norm_scale.at(i, l + 1))
                pool.tensor_tensor(shift[s][:, :], minus_mean[s][:, :], rstd[s][:, :], ALU.mult).then_inc(norm_ready[s], 1)

            def split_lo(i, s, what, b):
                pool.wait_ge(hi_part[s], hi_part.at(i, split_of(what, b) + 1))
                pool.tensor_tensor(h_nat_lo[s][:, b, :], h_nat[s][:, b, :], h_nat_hi[s][:, b, :], ALU.subtract).then_inc(lo_part[s], 1)

            def dst_diag_lo(i, s, a):
                pool.wait_ge(steps_done[s], steps_done.at(i, VECTOR_STEPS[3 * a] + 3))
                pool.tensor_tensor(dst_diag[s][:, 1, :, :], ident_h[:, :].unsqueeze(1).to_broadcast([P, GROUP, P]),
                                   dst_h[s][:, 1, :].unsqueeze(2).to_broadcast([P, GROUP, P]), ALU.mult).then_inc(diag_lo[s], 1)

            def probs_lo(i, s, a):
                pool.wait_ge(hi_part[s], hi_part.at(i, SPLIT[("probs0", "probs3")[a]] + 1))
                pool.wait_ge(full[s], full.at(i, SPLIT[("probs0", "probs3")[a]] + 1))
                pool.tensor_tensor(prob_lo[s][:, 0, 0:GROUP * P], prob[s][:, 0, 0:GROUP * P], prob_hi[s][:, 0, 0:GROUP * P],
                                   ALU.subtract).then_inc(lo_part[s], 1)

            def query_key_lo(i, s, j):
                pool.wait_ge(hi_part[s], hi_part.at(i, SPLIT["qk"] + j + 1))
                pool.wait_ge(full[s], full.at(i, SPLIT["qk"] + j + 1))
                pool.tensor_tensor(wide_lo[s][:, j, :], wide[s][:, j, :], wide_hi[s][:, j, :], ALU.subtract).then_inc(lo_part[s], 1)

            def heads_lo(i, s, b, k):
                pool.wait_ge(hi_part[s], hi_part.at(i, SPLIT["heads"] + HEAD_SPLITS * b + k + 1))
                pool.tensor_tensor(prob_lo[s][:, k, :], prob[s][:, k, :], prob_hi[s][:, k, :], ALU.subtract).then_inc(lo_part[s], 1)

            def slot(at):
                at(2, query_key_lo, 1)
                at(4, dst_diag_lo, 1)
                at(1, norm_pow, 1)
                at(2, query_key_lo, 2)
                at(1, norm_shift, 1)
                at(2, query_key_lo, 3)
                at(0, norm_pow, 0)
                at(1, split_lo, "h1", 0)
                at(0, norm_shift, 0)
                at(1, split_lo, "h1", 1)
                at(4, probs_lo, 1)
                at(0, split_lo, "h0", 0)
                at(3, split_lo, "out", 1)
                at(2, heads_lo, 0, 0)
                at(0, split_lo, "h0", 1)
                at(2, heads_lo, 0, 1)
                at(1, norm_pow, 2)
                at(1, norm_shift, 2)
                at(0, dst_diag_lo, 0)
                at(3, norm_pow, 3)
                at(3, norm_shift, 3)
                at(1, split_lo, "h2", 0)
                at(1, split_lo, "h2", 1)
                at(3, split_lo, "h3", 0)
                at(3, split_lo, "h3", 1)
                at(0, probs_lo, 0)
                at(2, split_lo, "out", 0)
                at(2, heads_lo, 1, 0)
                at(2, heads_lo, 1, 1)
                at(1, query_key_lo, 0)
            run(pool, slot)


def kernel(x, adj, L0_gnn_W, L0_gnn_a, L1_gnn_W, L1_gnn_b, L2_gnn_Wq, L2_gnn_bq, L2_gnn_Wk, L2_gnn_bk,
           L2_gnn_Wv, L2_gnn_bv, L2_gnn_Wo, L2_gnn_bo, L3_gnn_W, L3_gnn_a_src, L3_gnn_a_dst):
    import numpy as np
    import concourse.bacc as bacc
    from concourse.bass_utils import run_bass_kernel_spmd

    x, adj, w0, a0, w1, b1, wq, bq, wk, bk, wv, bv, wo, bo, w3, a_src, a_dst = (
        np.asarray(v) for v in (x, adj, L0_gnn_W, L0_gnn_a, L1_gnn_W, L1_gnn_b, L2_gnn_Wq, L2_gnn_bq, L2_gnn_Wk,
                                L2_gnn_bk, L2_gnn_Wv, L2_gnn_bv, L2_gnn_Wo, L2_gnn_bo, L3_gnn_W, L3_gnn_a_src,
                                L3_gnn_a_dst))
    columns = lambda v: v.reshape(-1, P).T
    arrays = {
        "in_x": x, "in_adj": adj, "in_adj_t": adj.T,
        "in_w0": w0, "in_w0_t": w0.T, "in_a0": a0[:, :, 0].T,
        "in_w_i": w1[:, :D].T, "in_w_j": w1[:, D:].T, "in_b1": b1,
        "in_w_q": wq.T, "in_w_k": wk.T, "in_b_qk": np.concatenate([columns(bq), columns(bk)], axis=1),
        "in_w_v": wv.T, "in_b_v": columns(bv), "in_w_o": wo.T, "in_b_o": bo,
        "in_w3": w3, "in_w3_t": w3.T, "in_a3": np.stack([a_src, a_dst], axis=1),
    }
    arrays = {k: np.ascontiguousarray(v) for k, v in arrays.items()}
    nc = bacc.Bacc("TRN2", target_bir_lowering=False, num_devices=1)
    args = [nc.dram_tensor(k, v.shape, mybir.dt.from_np(v.dtype), kind="ExternalInput").ap() for k, v in arrays.items()]
    out = nc.dram_tensor("out", x.shape, F32, kind="ExternalOutput").ap()
    nc.disable_value_cache = True
    build(nc, *args, out)
    return run_bass_kernel_spmd(nc, [arrays], core_ids=[0]).results[0]["out"]
```
